# Optimizing a Trainium2 kernel written in Bass

```python
import numpy as np
import jax
import jax.numpy as jnp

def _softmax(x, axis=-1):
    return jax.nn.softmax(x, axis=axis)

def _gelu(x):
    return jax.nn.gelu(x, approximate=True)

def _silu(x):
    return jax.nn.silu(x)

def _sigmoid(x):
    return jax.nn.sigmoid(x)

def _layernorm(x, axis=-1, eps=1e-05):
    m = jnp.mean(x, axis=axis, keepdims=True)
    v = jnp.var(x, axis=axis, keepdims=True)
    return (x - m) / jnp.sqrt(v + eps)

def _scatter_add(tgt, idx, src, axis=0):
    return tgt.at[idx].add(src)

def _segment_sum(src, seg, n):
    return jax.ops.segment_sum(src, seg, n)
kernel_name = 'mk_xattn_ffn_d1_seqx_r4_3b8b4e'

def setup_inputs(seed: int=0):
    np.random.seed(seed)
    _w = jnp.asarray

    def _rec_inputs():
        import jax
        import jax.numpy as jnp
        _rk = jax.random.key(seed)
        x = 7.22e-05 + 1 * jax.random.normal(jax.random.fold_in(_rk, 1), (64, 128, 512), jnp.float32)
        _lenS = 128 - jax.random.randint(jax.random.fold_in(_rk, 7), (64,), 0, max(1, 128 // 4) + 1, jnp.int32)
        _lenS2 = 128 - jax.random.randint(jax.random.fold_in(_rk, 8), (64,), 0, max(1, 128 // 4) + 1, jnp.int32)
        _ctx_1024P = jax.random.normal(jax.random.fold_in(_rk, 11), (64, 16, 256), jnp.float32)
        _ctx_1024c = jax.random.dirichlet(jax.random.fold_in(_rk, 511), 0.3 * jnp.ones((16,), jnp.float32), (64, 128))
        _ctx_1024t = jnp.einsum('bsk,bkd->bsd', _ctx_1024c, _ctx_1024P)
        _ctx_1024t = _ctx_1024t * jax.lax.rsqrt(jnp.mean(jnp.square(_ctx_1024t)) + 1e-12) * 0.953939
        ctx_1024 = -1.39393e-06 + 0.999914 * (_ctx_1024t + 0.3 * jax.random.normal(jax.random.fold_in(_rk, 611), (64, 128, 256), jnp.float32))
        fside_BxSx2_0 = jax.random.uniform(jax.random.fold_in(_rk, 12), (64, 128, 2), jnp.float32, 0.0, 0.999707)
        return (x, ctx_1024, fside_BxSx2_0)
    x, ctx_1024, fside_BxSx2_0 = _rec_inputs()

    def _L0_xattn_setup():
        import jax, jax.numpy as jnp
        import numpy as np
        DIM = 512
        CTX_DIM = 256
        N_HEADS = 32
        HEAD_DIM = DIM // N_HEADS
        POS_DIM = 2
        B, N, CTXN = (2, 512, 512)
        ROPE_BASE = 10000.0

        def apply_axial_rope(x, pos):
            b, n, h, d = x.shape
            p = pos.shape[-1]
            dpa = d // p
            half = dpa // 2
            freqs = ROPE_BASE ** (-jnp.arange(half, dtype=x.dtype) / half)
            ang = pos[..., :, None] * freqs
            cos = jnp.cos(ang)[:, :, None, :, :]
            sin = jnp.sin(ang)[:, :, None, :, :]
            xr = x.reshape(b, n, h, p, half, 2)
            x1, x2 = (xr[..., 0], xr[..., 1])
            out = jnp.stack([x1 * cos - x2 * sin, x1 * sin + x2 * cos], axis=-1)
            return out.reshape(b, n, h, d)
        key = jax.random.key(seed)
        ks = jax.random.split(key, 8)
        x = jax.random.normal(ks[0], (B, N, DIM), jnp.float32)
        ctx = jax.random.normal(ks[1], (B, CTXN, CTX_DIM), jnp.float32)
        pos_map = jax.random.uniform(ks[2], (B, N, POS_DIM), jnp.float32)
        ctx_pos_map = jax.random.uniform(ks[3], (B, CTXN, POS_DIM), jnp.float32)
        Wq = jax.random.normal(ks[4], (DIM, DIM), jnp.float32) / np.sqrt(DIM)
        Wkv = jax.random.normal(ks[5], (CTX_DIM, 2 * DIM), jnp.float32) / np.sqrt(CTX_DIM)
        Wout = jax.random.normal(ks[6], (DIM, DIM), jnp.float32) / np.sqrt(DIM)
        bout = jnp.zeros((DIM,), jnp.float32)
        return {'x': x, 'ctx': ctx, 'pos_map': pos_map, 'ctx_pos_map': ctx_pos_map, 'Wq': Wq, 'Wkv': Wkv, 'Wout': Wout, 'bout': bout}
    _L0_xattn_all = _L0_xattn_setup()
    _L0_xattn_in = {k: v for k, v in _L0_xattn_all.items() if k in ('Wq', 'Wkv', 'Wout', 'bout')}
    del _L0_xattn_all

    def _L0_ffn_setup():
        import jax, jax.numpy as jnp
        import numpy as np
        _FP4_LUT = jnp.array([0.0, 0.5, 1.0, 1.5, 2.0, 3.0, 4.0, 6.0, -0.0, -0.5, -1.0, -1.5, -2.0, -3.0, -4.0, -6.0], dtype=jnp.float32)
        GROUP_SIZE = 128
        EPS = 1e-06

        def _dequant_fp4(packed_i32, scales_f16, group_size):
            out_f, in_p = packed_i32.shape
            w = packed_i32.astype(jnp.uint32)
            shifts = jnp.arange(8, dtype=jnp.uint32) * 4
            nib = w[:, :, None] >> shifts & jnp.uint32(15)
            vals = _FP4_LUT[nib.astype(jnp.int32)].reshape(out_f, in_p * 8)
            s = scales_f16.astype(jnp.float32).T
            s_full = jnp.repeat(s, group_size, axis=1)
            return vals * s_full
        key = jax.random.key(seed)
        k1, k2, k3, k4, k5 = jax.random.split(key, 5)
        B, S, H, I = (4, 512, 512, 1408)
        x = jax.random.normal(k1, (B, S, H), dtype=jnp.float32)
        gate_up_packed = jax.random.randint(k2, (2 * I, H // 8), 0, 2147483647, dtype=jnp.int32)
        gate_up_scales = jax.random.uniform(k3, (H // GROUP_SIZE, 2 * I), dtype=jnp.float32).astype(jnp.float16)
        down_packed = jax.random.randint(k4, (H, I // 8), 0, 2147483647, dtype=jnp.int32)
        down_scales = jax.random.uniform(k5, (I // GROUP_SIZE, H), dtype=jnp.float32).astype(jnp.float16)
        return {'x': x, 'gate_up_packed': gate_up_packed, 'gate_up_scales': gate_up_scales, 'down_packed': down_packed, 'down_scales': down_scales}
    _L0_ffn_all = _L0_ffn_setup()
    _L0_ffn_in = {k: v for k, v in _L0_ffn_all.items() if k in ('gate_up_packed', 'gate_up_scales', 'down_packed', 'down_scales')}
    del _L0_ffn_all
    return {'x': x, 'ctx_1024': ctx_1024, 'fside_BxSx2_0': fside_BxSx2_0, 'L0_xattn_Wq': _L0_xattn_in['Wq'], 'L0_xattn_Wkv': _L0_xattn_in['Wkv'], 'L0_xattn_Wout': _L0_xattn_in['Wout'], 'L0_xattn_bout': _L0_xattn_in['bout'], 'L0_ffn_gate_up_packed': _L0_ffn_in['gate_up_packed'], 'L0_ffn_gate_up_scales': _L0_ffn_in['gate_up_scales'], 'L0_ffn_down_packed': _L0_ffn_in['down_packed'], 'L0_ffn_down_scales': _L0_ffn_in['down_scales']}

def reference(x, ctx_1024, fside_BxSx2_0, L0_xattn_Wq, L0_xattn_Wkv, L0_xattn_Wout, L0_xattn_bout, L0_ffn_gate_up_packed, L0_ffn_gate_up_scales, L0_ffn_down_packed, L0_ffn_down_scales):
    import jax
    import jax.numpy as jnp

    def _L0_xattn_ref(x, ctx, pos_map, ctx_pos_map, Wq, Wkv, Wout, bout):
        import jax, jax.numpy as jnp
        import numpy as np
        DIM = 512
        CTX_DIM = 256
        N_HEADS = 32
        HEAD_DIM = DIM // N_HEADS
        POS_DIM = 2
        B, N, CTXN = (2, 512, 512)
        ROPE_BASE = 10000.0

        def apply_axial_rope(x, pos):
            b, n, h, d = x.shape
            p = pos.shape[-1]
            dpa = d // p
            half = dpa // 2
            freqs = ROPE_BASE ** (-jnp.arange(half, dtype=x.dtype) / half)
            ang = pos[..., :, None] * freqs
            cos = jnp.cos(ang)[:, :, None, :, :]
            sin = jnp.sin(ang)[:, :, None, :, :]
            xr = x.reshape(b, n, h, p, half, 2)
            x1, x2 = (xr[..., 0], xr[..., 1])
            out = jnp.stack([x1 * cos - x2 * sin, x1 * sin + x2 * cos], axis=-1)
            return out.reshape(b, n, h, d)
        b, n, _ = x.shape
        ctx_n = ctx.shape[1]
        q = (x @ Wq).reshape(b, n, N_HEADS, HEAD_DIM)
        k, v = jnp.split(ctx @ Wkv, 2, axis=-1)
        k = k.reshape(b, ctx_n, N_HEADS, HEAD_DIM)
        v = v.reshape(b, ctx_n, N_HEADS, HEAD_DIM)
        q = apply_axial_rope(q, pos_map)
        k = apply_axial_rope(k, ctx_pos_map)
        scale = 1.0 / np.sqrt(HEAD_DIM).astype(np.float32)
        logits = jnp.einsum('bqhd,bkhd->bhqk', q, k) * scale
        w = jax.nn.softmax(logits, axis=-1)
        attn = jnp.einsum('bhqk,bkhd->bqhd', w, v)
        attn = attn.reshape(b, n, N_HEADS * HEAD_DIM)
        return attn @ Wout + bout

    def _L0_ffn_ref(x, gate_up_packed, gate_up_scales, down_packed, down_scales):
        import jax, jax.numpy as jnp
        import numpy as np
        _FP4_LUT = jnp.array([0.0, 0.5, 1.0, 1.5, 2.0, 3.0, 4.0, 6.0, -0.0, -0.5, -1.0, -1.5, -2.0, -3.0, -4.0, -6.0], dtype=jnp.float32)
        GROUP_SIZE = 128
        EPS = 1e-06

        def _dequant_fp4(packed_i32, scales_f16, group_size):
            out_f, in_p = packed_i32.shape
            w = packed_i32.astype(jnp.uint32)
            shifts = jnp.arange(8, dtype=jnp.uint32) * 4
            nib = w[:, :, None] >> shifts & jnp.uint32(15)
            vals = _FP4_LUT[nib.astype(jnp.int32)].reshape(out_f, in_p * 8)
            s = scales_f16.astype(jnp.float32).T
            s_full = jnp.repeat(s, group_size, axis=1)
            return vals * s_full
        I = gate_up_packed.shape[0] // 2
        w_gu = _dequant_fp4(gate_up_packed, gate_up_scales, GROUP_SIZE)
        w_down = _dequant_fp4(down_packed, down_scales, GROUP_SIZE)
        gate_up = jnp.einsum('bsh,oh->bso', x, w_gu)
        gate, up = (gate_up[..., :I], gate_up[..., I:])
        h = jax.nn.silu(gate) * up
        y = jnp.einsum('bsi,hi->bsh', h, w_down)
        rms = jnp.sqrt(jnp.mean(y * y, axis=-1, keepdims=True) + EPS)
        return y / rms
    x = x + _L0_xattn_ref(_layernorm(x, axis=-1), ctx_1024, fside_BxSx2_0, fside_BxSx2_0, L0_xattn_Wq, L0_xattn_Wkv, L0_xattn_Wout, L0_xattn_bout)
    x = x + _L0_ffn_ref(_layernorm(x, axis=-1), L0_ffn_gate_up_packed, L0_ffn_gate_up_scales, L0_ffn_down_packed, L0_ffn_down_scales)
    return x

_drawn_inputs = setup_inputs


def setup_inputs(seed=0):
    import zlib

    import numpy as np

    out = dict(_drawn_inputs(seed))
    spreads = {'L0_xattn_bout': (0.0, 0.1)}
    factors = {}
    for name, (base, spread) in spreads.items():
        noise = np.random.default_rng([zlib.crc32(name.encode()), seed]).standard_normal(out[name].shape)
        drawn = base * np.exp(spread * noise) if base else spread * noise
        out[name] = jnp.asarray(drawn.astype(out[name].dtype))
    for name, factor in factors.items():
        out[name] = (out[name] * factor).astype(out[name].dtype)
    return out
```

```python
import concourse.bass as bass
from concourse import mybir
from contextlib import ExitStack

F32 = mybir.dt.float32
F32R = mybir.dt.float32r
F16 = mybir.dt.float16
U32 = mybir.dt.uint32
ALU = mybir.AluOpType
ACT = mybir.ActivationFunctionType
AX = mybir.AxisListType

P = 128
DIM = 512
CTX = 256
HEADS = 32
HD = DIM // HEADS
INTER = 1408
GROUP = 128
KD = DIM // P
KC = CTX // P
KI = INTER // P
HPT = P // HD
UNITS = HEADS // 4
LN_EPS = 1e-5
RMS_EPS = 1e-6
CHUNK = 4

TWO_PI = 6.283185307179586
PI_A = 6.28125
PI_B = 0.0019340515136718750
PI_C = TWO_PI - PI_A - PI_B
ROUND = 12582912.0
PI_IN = 3.1415925


class Named:
    pass


def wait(engine, semaphore, value):
    if not isinstance(value, int) or value > 0:
        engine.wait_ge(semaphore, value)


def setup_constants(nc, sem, c, tmp, A_pos, A_wq, A_wkv, A_wo, A_bout, tiles):
    with nc.Block() as block:

        @block.sync
        def _(sp):
            sp.dma_start(tmp.pos[:, :, :], A_pos.rearrange("t p a -> p t a")).then_inc(sem.pos_loaded, 16)
            sp.dma_start(tmp.wq[:, :, :], A_wq.rearrange("(k p) n -> p k n", p=P)).then_inc(sem.wq_loaded, 16)
            sp.dma_start(tmp.wkv[:, :, :], A_wkv.rearrange("(k p) n -> p k n", p=P)).then_inc(sem.wkv_loaded, 16)
            sp.dma_start(tmp.wo[:, :, :], A_wo.rearrange("(k p) n -> p k n", p=P)).then_inc(sem.wo_loaded, 16)
            sp.dma_start(c.bout[:, :], A_bout.rearrange("(a n) -> a n", a=1).broadcast_to([P, DIM])).then_inc(
                sem.bout_loaded, 16)
            sp.wait_ge(sem.bout_loaded, 16)

        @block.gpsimd
        def _(pool):
            pool.memset(c.ident[:, :], 0.0).then_inc(sem.const_set, 1)
            pool.memset(c.ident16[:, :], 0.0).then_inc(sem.const_set, 1)
            pool.memset(c.minus_half[:, :], -0.5).then_inc(sem.const_set, 1)
            pool.memset(c.ln_eps[:, :], LN_EPS).then_inc(sem.const_set, 1)
            pool.memset(c.rms_eps[:, :], RMS_EPS).then_inc(sem.const_set, 1)
            pool.wait_ge(sem.const_set, 5)
            for ident in (c.ident, c.ident16):
                pool.affine_select(out=ident[:, :], in_=ident[:, :], compare_op=ALU.not_equal, fill=1.0, base=0,
                                   pattern=[[-1, P]], channel_multiplier=1).then_inc(sem.const_set, 1)

        def permuted(w):
            return w.rearrange("p k (h i e) -> p k h e i", e=2, i=HD // 2)

        def plain(w):
            return w.rearrange("p k (h e i) -> p k h e i", e=2, i=HD // 2)

        def parts():
            for k in range(KD):
                yield sem.wq_loaded, tmp.wq[:, k:k + 1, :], (c.wq[0][:, k:k + 1, :], c.wq[1][:, k:k + 1, :]), True
            for k in range(KC):
                yield (sem.wkv_loaded, tmp.wkv[:, k:k + 1, 0:DIM],
                       (c.wkv[0][:, k:k + 1, 0:DIM], c.wkv[1][:, k:k + 1, 0:DIM]), True)
                yield (sem.wkv_loaded, tmp.wkv[:, k:k + 1, DIM:2 * DIM],
                       (c.wkv[0][:, k:k + 1, DIM:2 * DIM], c.wkv[1][:, k:k + 1, DIM:2 * DIM]), False)
            for k in range(KD):
                yield sem.wo_loaded, tmp.wo[:, k:k + 1, :], (c.wo[0][:, k:k + 1, :], c.wo[1][:, k:k + 1, :]), False

        @block.scalar
        def _(act):
            for loaded, src, (hi, _), permute in parts():
                act.wait_ge(loaded, 16)
                s, d = (permuted(src), plain(hi)) if permute else (src, hi)
                act.activation(d[:, 0], s[:, 0], ACT.Copy).then_inc(sem.w_hi, 1)
            act.wait_ge(sem.angles, 1)
            act.activation(c.sin[:, :, 0, :], tmp.ang_s[:, :, :], ACT.Sin, scale=-1.0)
            act.activation(c.sin[:, :, 1, :], tmp.ang_s[:, :, :], ACT.Sin)
            act.activation(c.cos[:, :, 0, :], tmp.ang_c[:, :, :], ACT.Sin)
            act.activation(c.cos[:, :, 1, :], tmp.ang_c[:, :, :], ACT.Sin).then_inc(sem.tables, 1)
            act.wait_ge(sem.tables, 1)

        @block.vector
        def _(dve):
            steps = [0]

            def then(ins):
                steps[0] += 1
                ins.then_inc(sem.setup_chain, 1)
                dve.wait_ge(sem.setup_chain, steps[0])

            dve.wait_ge(sem.pos_loaded, 16)
            ang, n, r = tmp.ang, tmp.turns, (tmp.ang_s, tmp.ang_c)
            for f in range(4):
                last = dve.tensor_scalar(ang[:, :, :].rearrange("p t (a f) -> p t a f", f=4)[:, :, :, f],
                                         tmp.pos[:, :, :], float(10000.0 ** (-f / 4.0)), None, ALU.mult)
            then(last)
            for i, (quarter, shift) in enumerate(((0.0, 0.0), (0.25, TWO_PI / 4))):
                then(dve.tensor_scalar(n[:, :, :], ang[:, :, :], 1 / TWO_PI, quarter, ALU.mult, ALU.add))
                then(dve.tensor_scalar(n[:, :, :], n[:, :, :], ROUND, ROUND, ALU.add, ALU.subtract))
                src = ang
                for part in (PI_A, PI_B, PI_C):
                    then(dve.scalar_tensor_tensor(out=r[i][:, :, :], in0=n[:, :, :], scalar=-part,
                                                  in1=src[:, :, :], op0=ALU.mult, op1=ALU.add))
                    src = r[i]
                then(dve.tensor_scalar(r[i][:, :, :], r[i][:, :, :], shift, PI_IN, ALU.add, ALU.min))
                then(dve.tensor_scalar(r[i][:, :, :], r[i][:, :, :], -PI_IN, None, ALU.max))
            dve.sem_inc(sem.angles, 1)
            for n_part, (loaded, src, (hi, lo), permute) in enumerate(parts()):
                dve.wait_ge(loaded, 16)
                dve.wait_ge(sem.w_hi, n_part + 1)
                s, h, d = ((permuted(src), plain(hi.bitcast(F32)), plain(lo)) if permute
                           else (src, hi.bitcast(F32), lo))
                dve.tensor_tensor(d[:, 0], s[:, 0], h[:, 0], ALU.subtract).then_inc(sem.w_lo, 1)


def attention(nc, sem, c, b, ps, A_x, A_ctx, x1_dram, tiles):
    S, ET, AV, MA, MB = ps.scores, ps.et, ps.av, ps.misc_a, ps.misc_b

    def steps(step, engine):
        for t in range(4):
            step(t, t // 2, t % 2)
        with engine.Fori(2, tiles // 2 - 1) as r:
            step(2 * r, r, 0)
            step(2 * r + 1, r, 1)
        step(tiles - 2, tiles // 2 - 1, 0)
        step(tiles - 1, tiles // 2 - 1, 1)
        step(tiles, tiles // 2, 0)

    def stages(t):
        if isinstance(t, int):
            return t >= 1, t < tiles, t + 1 < tiles, t + 2 < tiles
        return True, True, True, True

    with nc.Block() as block:

        @block.sync
        def _(sp):
            def load_x(m, r, par):
                sp.dma_start(b.x[par][:, :], A_x[bass.ds(m, 1), :, :].rearrange("a p n -> p (a n)")).then_inc(
                    sem.x_loaded[par], 16)

            def load_ctx(m, r, par):
                sp.dma_start(b.ctx[par][:, :], A_ctx[bass.ds(m, 1), :, :].rearrange("a p n -> p (a n)")).then_inc(
                    sem.ctx_loaded[par], 16)

            def spread_k(n, r, par):
                sp.wait_ge(sem.klo_done, n + 1)
                wait(sp, sem.s_done, 4 * n - 4)
                for j in range(HPT):
                    rows = slice(HD * j, HD * (j + 1))
                    sp.dma_start(b.kblk[par][rows, :, :, j, :].bitcast(F32),
                                 b.kT[rows, :, :, :].bitcast(F32)).then_inc(sem.kblk_ready[par], 16)

            load_x(0, 0, 0)
            load_ctx(0, 0, 0)
            load_x(1, 0, 1)
            load_ctx(1, 0, 1)
            sp.wait_ge(sem.kblk_zeroed, 2)
            spread_k(0, 0, 0)

            def step(t, r, par):
                tail, own, front, ahead = stages(t)
                if ahead:
                    sp.wait_ge(sem.ctxT_done, t + 1)
                    load_ctx(t + 2, r + 1, par)
                    sp.wait_ge(sem.xb_done, t + 1)
                    load_x(t + 2, r + 1, par)
                if front:
                    spread_k(t + 1, r + par, 1 - par)
                if tail:
                    sp.wait_ge(sem.x1_done, t)
                    sp.dma_start(x1_dram[bass.ds(t - 1, 1), :, :].rearrange("a p n -> p (a n)"),
                                 b.x1[1 - par][:, :]).then_inc(sem.x1_stored[1 - par], 16)

            steps(step, sp)
            for par in range(2):
                sp.wait_ge(sem.x1_stored[par], 16 * (tiles // 2))

        @block.gpsimd
        def _(pool):
            def rstd(m):
                pool.wait_ge(sem.stats_done, m + 1)
                pool.tensor_tensor(b.rstd[:, :], b.mv[:, 1:2], c.ln_eps[:, :], ALU.add).then_inc(sem.vareps_done, 1)
                pool.wait_ge(sem.vareps_done, m + 1)
                pool.tensor_tensor(b.rstd[:, :], b.rstd[:, :], c.minus_half[:, :], ALU.pow).then_inc(sem.rstd_done, 1)

            def rope_add(n, which, products_done, rotated, transposed_done, added):
                pool.wait_ge(products_done, n + 1)
                wait(pool, transposed_done, n)
                pool.tensor_tensor(rotated[:, :], b.rope[which][0][:, :], b.rope[which][1][:, :],
                                   ALU.add).then_inc(added, 1)

            def rope_add_k(n):
                rope_add(n, 0, sem.kmul_done, b.kr, sem.kT_done, sem.kr_done)

            def rope_add_q(n):
                rope_add(n, 1, sem.qmul_done, b.qr, sem.qT_done, sem.qr_done)

            for par in range(2):
                pool.memset(b.v[par][:, :, :], 0.0).then_inc(sem.v_zeroed, 1)
            pool.wait_ge(sem.v_zeroed, 2)
            for par in range(2):
                pool.memset(b.v[par][:, :, HD:HD + 1], 1.0).then_inc(sem.v_ones, 1)
            rstd(0)
            rope_add_k(0)
            rstd(1)
            rope_add_q(0)

            def step(t, r, par):
                tail, own, front, ahead = stages(t)
                if own:
                    wait(pool, sem.x1_done, t - 1)
                    pool.wait_ge(sem.x_loaded[par], 16 * (r + 1))
                    pool.tensor_tensor(b.xb[par][:, :], b.x[par][:, :], c.bout[:, :], ALU.add).then_inc(sem.xb_done, 1)
                if front:
                    rope_add_k(t + 1)
                if ahead:
                    rstd(t + 2)
                if front:
                    rope_add_q(t + 1)

            steps(step, pool)

        @block.scalar
        def _(act):
            def ctx_hi(n):
                act.wait_ge(sem.ctxT_done, n + 1)
                wait(act, sem.v_done, n)
                act.activation(b.cT[0][:, :, :], MB[:, 0:CTX].rearrange("p (k n) -> p k n", k=KC),
                               ACT.Copy).then_inc(sem.chi_done, 1)

            def x_hi(n):
                act.wait_ge(sem.xT_done, n + 1)
                wait(act, sem.q_done, n)
                act.activation(b.xT[0][:, :, :], MB[:, :].rearrange("p (k n) -> p k n", k=KD),
                               ACT.Copy).then_inc(sem.xhi_done, 1)

            def k_hi(n, r, par):
                act.wait_ge(sem.kT_done, n + 1)
                wait(act, sem.kblk_ready[1 - par], 16 * HPT * (r + par))
                act.activation(b.kT[:, 0, :, :], MB[:, :].rearrange("p (k n) -> p k n", k=KD),
                               ACT.Copy).then_inc(sem.khi_done, 1)

            def q_hi(n, par):
                act.wait_ge(sem.qT_done, n + 1)
                wait(act, sem.s_done, 4 * n - 4)
                act.activation(b.qT[par][0][:, :, :], MA[:, :].rearrange("p (k n) -> p k n", k=KD),
                               ACT.Copy).then_inc(sem.qhi_done, 1)

            def v_copy(n, par):
                act.wait_ge(sem.v_done, n + 1)
                wait(act, sem.av_done, UNITS * (n - 1))
                act.activation(b.v[par][:, :, 0:HD], MB[:, :].rearrange("p (h d) -> p h d", d=HD),
                               ACT.Copy).then_inc(sem.v_copied, 1)

            def exps(t, g):
                G = 4 * t + g
                act.wait_ge(sem.sub_done, G + 1)
                act.activation(b.e[g % 2][:, :], b.e[g % 2][:, :], ACT.Exp, scale=HD ** -0.5).then_inc(sem.exp_done, 1)

            def et_copy(t, u):
                U = UNITS * t + u
                act.wait_ge(sem.et_done, U + 1)
                wait(act, sem.av_done, U - 1)
                act.activation(b.et[u % 2][:, :], ET[:, :], ACT.Copy).then_inc(sem.et_copied, 1)

            def av_copy(t, half):
                H = 2 * t + half
                act.wait_ge(sem.av_done, 4 * H + 4)
                wait(act, sem.outT_done, H - 1)
                act.activation(b.avT[half][:, :], AV[:, :], ACT.Copy).then_inc(sem.av_copied, 1)

            def attn_hi(p):
                act.wait_ge(sem.attnT_done, p + 1)
                wait(act, sem.o_done, p)
                act.activation(b.aT[0][:, :, :], MB[:, :].rearrange("p (k n) -> p k n", k=KD),
                               ACT.Copy).then_inc(sem.ahi_done, 1)

            ctx_hi(0)
            x_hi(0)
            k_hi(0, 0, 0)
            act.wait_ge(sem.v_ones, 2)
            v_copy(0, 0)
            ctx_hi(1)
            q_hi(0, 0)
            exps(0, 0)

            def step(t, r, par):
                tail, own, front, ahead = stages(t)
                n, p = t + 1, t - 1
                if own:
                    et_copy(t, 0)
                if tail:
                    av_copy(p, 1)
                if own:
                    et_copy(t, 1)
                    exps(t, 1)
                if front:
                    x_hi(n)
                if own:
                    et_copy(t, 2)
                if front:
                    k_hi(n, r + par, 1 - par)
                if own:
                    et_copy(t, 3)
                    exps(t, 2)
                    et_copy(t, 4)
                    av_copy(t, 0)
                if tail:
                    attn_hi(p)
                if own:
                    et_copy(t, 5)
                    exps(t, 3)
                if front:
                    q_hi(n, 1 - par)
                if own:
                    et_copy(t, 6)
                if front:
                    v_copy(n, 1 - par)
                if own:
                    et_copy(t, 7)
                if ahead:
                    ctx_hi(n + 1)
                if front:
                    exps(n, 0)

            steps(step, act)

        @block.vector
        def _(dve):
            def stats(m, r, par):
                dve.wait_ge(sem.x_loaded[par], 16 * (r + 1))
                dve.bn_stats(b.bn[:, :], b.x[par][:, :]).then_inc(sem.bn_done, 1)

            def mean_variance():
                dve.bn_aggr(b.mv[:, :], b.bn[:, :]).then_inc(sem.stats_done, 1)

            def normalise(m, par):
                dve.wait_ge(sem.rstd_done, m + 1)
                wait(dve, sem.xT_done, m)
                dve.tensor_scalar(b.xn[:, :], b.x[par][:, :], b.mv[:, 0:1], b.rstd[:, 0:1], ALU.subtract,
                                  ALU.mult).then_inc(sem.xn_done, 1)

            def low_part(source, high, low, high_done, n, low_done):
                dve.wait_ge(high_done, n + 1)
                dve.tensor_tensor(low, source, high.bitcast(F32), ALU.subtract).then_inc(low_done, 1)

            def tiled(bank, k=KD):
                return bank[:, 0:k * P].rearrange("p (k n) -> p k n", k=k)

            def ctx_lo(n):
                low_part(tiled(MB, KC), b.cT[0][:, :, :], b.cT[1][:, :, :], sem.chi_done, n, sem.clo_done)

            def x_lo(n):
                low_part(tiled(MB), b.xT[0][:, :, :], b.xT[1][:, :, :], sem.xhi_done, n, sem.xlo_done)

            def k_lo(n):
                low_part(tiled(MB), b.kT[:, 0, :, :], b.kT[:, 1, :, :], sem.khi_done, n, sem.klo_done)

            def q_lo(n, par):
                low_part(tiled(MA), b.qT[par][0][:, :, :], b.qT[par][1][:, :, :], sem.qhi_done, n, sem.qlo_done)

            def attn_lo(p):
                low_part(tiled(MB), b.aT[0][:, :, :], b.aT[1][:, :, :], sem.ahi_done, p, sem.alo_done)

            def rope_products(bank, n, which, projected, added, done):
                dve.wait_ge(projected, n + 1)
                wait(dve, added, n)
                table = (c.cos, c.sin)
                cos, sin = (x[:, bass.ds(n, 1), :, :].rearrange("p a e i -> p a (e i)").broadcast_to([P, HEADS, HD])
                            for x in table)
                dve.tensor_tensor(b.rope[which][0][:, :].rearrange("p (h d) -> p h d", d=HD),
                                  bank[:, :].rearrange("p (h d) -> p h d", d=HD), cos, ALU.mult)
                swapped = bank[:, :].rearrange("p (h e i) -> p h e i", e=2, i=HD // 2)[:, :, ::-1, :]
                dve.tensor_tensor(b.rope[which][1][:, :].rearrange("p (h e i) -> p h e i", e=2, i=HD // 2),
                                  swapped, sin.rearrange("p h (e i) -> p h e i", e=2), ALU.mult).then_inc(done, 1)

            def rope_k(n):
                rope_products(MA, n, 0, sem.k_done, sem.kr_done, sem.kmul_done)

            def rope_q(n):
                rope_products(MA, n, 1, sem.q_done, sem.qr_done, sem.qmul_done)

            def softmax_shift(t, g):
                G = 4 * t + g
                bank = S[g % 2][:, :].rearrange("p (h k) -> p h k", k=P)
                dve.wait_ge(sem.s_done, G + 1)
                dve.reduce_max(b.mx[g % 2][:, :], bank, AX.X).then_inc(sem.mx_done, 1)
                dve.wait_ge(sem.mx_done, G + 1)
                wait(dve, sem.et_done, 2 * G - 2)
                dve.tensor_tensor(b.e[g % 2][:, :].rearrange("p (h k) -> p h k", k=P), bank,
                                  b.mx[g % 2][:, :].unsqueeze(2).broadcast_to([P, HPT, P]),
                                  ALU.subtract).then_inc(sem.sub_done, 1)

            def divide(p, half):
                H = 2 * p + half
                bank = (MB, MA)[half][:, :].rearrange("p (h d) -> p h d", d=2 * HD)
                dve.wait_ge(sem.outT_done, H + 1)
                dve.reciprocal(b.rsum[half][:, :], bank[:, :, HD]).then_inc(sem.rsum_done, 1)
                dve.wait_ge(sem.rsum_done, H + 1)
                wait(dve, sem.attnT_done, p)
                dve.tensor_tensor(b.attn[:, half, :].rearrange("p (h d) -> p h d", d=HD), bank[:, :, 0:HD],
                                  b.rsum[half][:, :].unsqueeze(2).broadcast_to([P, HEADS // 2, HD]),
                                  ALU.mult).then_inc(sem.norm_done, 1)

            def residual(p, r, par):
                dve.wait_ge(sem.o_done, p + 1)
                dve.wait_ge(sem.xb_done, p + 1)
                wait(dve, sem.x1_stored[par], 16 * r)
                dve.tensor_tensor(b.x1[par][:, :], MA[:, :], b.xb[par][:, :], ALU.add).then_inc(sem.x1_done, 1)

            for par in range(2):
                dve.memset(b.kblk[par][:, :, :, :, :].rearrange("p a k j n -> p (a k j n)").bitcast(U32),
                           0).then_inc(sem.kblk_zeroed, 1)
            stats(0, 0, 0)
            dve.wait_ge(sem.bn_done, 1)
            mean_variance()
            normalise(0, 0)
            ctx_lo(0)
            rope_k(0)
            x_lo(0)
            stats(1, 0, 1)
            dve.wait_ge(sem.bn_done, 2)
            mean_variance()
            k_lo(0)
            rope_q(0)
            normalise(1, 1)
            ctx_lo(1)
            q_lo(0, 0)
            softmax_shift(0, 0)

            def step(t, r, par):
                tail, own, front, ahead = stages(t)
                n, p = t + 1, t - 1
                if own:
                    softmax_shift(t, 1)
                if tail:
                    divide(p, 0)
                if front:
                    rope_k(n)
                    x_lo(n)
                if tail:
                    divide(p, 1)
                if ahead:
                    stats(t + 2, r + 1, par)
                    dve.wait_ge(sem.bn_done, t + 3)
                if front:
                    k_lo(n)
                if ahead:
                    mean_variance()
                if own:
                    softmax_shift(t, 2)
                if front:
                    rope_q(n)
                if own:
                    softmax_shift(t, 3)
                if tail:
                    attn_lo(p)
                if front:
                    q_lo(n, 1 - par)
                    softmax_shift(n, 0)
                if ahead:
                    ctx_lo(n + 1)
                if tail:
                    residual(p, r + par - 1, 1 - par)
                if ahead:
                    normalise(t + 2, par)

            steps(step, dve)

        @block.tensor
        def _(pe):
            def product(out, pairs, done):
                for i, (w, m) in enumerate(pairs):
                    last = nc.tensor.matmul(out, w, m, start=(i == 0), stop=(i == len(pairs) - 1))
                last.then_inc(done, 1)

            def three(w, m, k_tiles):
                return [(w(i, k), m(j, k)) for i, j in ((0, 1), (1, 0), (0, 0)) for k in range(k_tiles)]

            def ctx_transpose(n, r, par):
                pe.wait_ge(sem.ctx_loaded[par], 16 * (r + 1))
                wait(pe, sem.v_copied, n)
                for k in range(KC):
                    last = nc.tensor.transpose(MB[:, k * P:(k + 1) * P], b.ctx[par][:, k * P:(k + 1) * P],
                                               c.ident[:, :])
                last.then_inc(sem.ctxT_done, 1)

            def transpose4(bank, src, done):
                for k in range(KD):
                    last = nc.tensor.transpose(bank[:, k * P:(k + 1) * P], src[:, k * P:(k + 1) * P], c.ident[:, :])
                last.then_inc(done, 1)

            def out_transpose(p, half, own, front):
                H = 2 * p + half
                pe.wait_ge(sem.av_copied, H + 1)
                if half == 0:
                    if front:
                        pe.wait_ge(sem.clo_done, p + 3)
                    elif own:
                        pe.wait_ge(sem.v_copied, p + 2)
                elif front:
                    pe.wait_ge(sem.kmul_done, p + 3)
                else:
                    pe.wait_ge(sem.x1_done, p)
                transpose4((MB, MA)[half], b.avT[half], sem.outT_done)

            def k_project(n):
                pe.wait_ge(sem.clo_done, n + 1)
                wait(pe, sem.x1_done, n - 2)
                product(MA[:, :], three(lambda i, k: b.cT[i][:, k, :], lambda i, k: c.wkv[i][:, k, 0:DIM], KC),
                        sem.k_done)

            def v_project(n, tail):
                if tail:
                    pe.wait_ge(sem.alo_done, n - 1)
                else:
                    pe.wait_ge(sem.klo_done, n + 1)
                product(MB[:, :], three(lambda i, k: b.cT[i][:, k, :], lambda i, k: c.wkv[i][:, k, DIM:2 * DIM], KC),
                        sem.v_done)

            def q_project(n, tail):
                pe.wait_ge(sem.xlo_done, n + 1)
                if tail:
                    pe.wait_ge(sem.norm_done, 2 * n - 2)
                else:
                    pe.wait_ge(sem.kmul_done, n + 1)
                product(MA[:, :], three(lambda i, k: b.xT[i][:, k, :], lambda i, k: c.wq[i][:, k, :], KD), sem.q_done)

            def x_transpose(n, tail):
                pe.wait_ge(sem.xn_done, n + 1)
                if tail:
                    pe.wait_ge(sem.norm_done, 2 * n - 3)
                else:
                    pe.wait_ge(sem.clo_done, n + 1)
                transpose4(MB, b.xn, sem.xT_done)

            def k_transpose(n):
                pe.wait_ge(sem.kr_done, n + 1)
                pe.wait_ge(sem.xlo_done, n + 1)
                transpose4(MB, b.kr, sem.kT_done)

            def q_transpose(n):
                pe.wait_ge(sem.qr_done, n + 1)
                transpose4(MA, b.qr, sem.qT_done)

            def scores(t, g, r, par):
                G = 4 * t + g
                wait(pe, sem.sub_done, G - 1)
                if g == 0:
                    pe.wait_ge(sem.kblk_ready[par], 16 * HPT * (r + 1))
                    pe.wait_ge(sem.qlo_done, t + 1)
                for half in range(2):
                    pairs = [(b.qT[par][i][:, g, :], b.kblk[par][:, j, g, 4 * half:4 * half + 4, :])
                             for i, j in ((0, 1), (1, 0), (0, 0))]
                    for i, (w, m) in enumerate(pairs):
                        last = nc.tensor.matmul(S[g % 2][:, 512 * half:512 * half + 512], w,
                                                m.rearrange("p h k -> p (h k)"), start=(i == 0), stop=(i == 2))
                last.then_inc(sem.s_done, 1)

            def e_transpose(t, u):
                U = UNITS * t + u
                if u % 2 == 0:
                    pe.wait_ge(sem.exp_done, 4 * t + u // 2 + 1)
                wait(pe, sem.et_copied, U)
                transpose4(ET, b.e[u // 2 % 2][:, 512 * (u % 2):512 * (u % 2) + 512], sem.et_done)

            def values(t, u, par):
                U = UNITS * t + u
                pe.wait_ge(sem.et_copied, U + 1)
                if u == 0:
                    pe.wait_ge(sem.v_copied, t + 1)
                if u % 4 == 0:
                    wait(pe, sem.av_copied, 2 * t + u // 4)
                for i in range(4):
                    last = nc.tensor.matmul(AV[32 * i:32 * i + 32, (u % 4) * P:(u % 4 + 1) * P],
                                            b.v[par][:, 4 * u + i, :], b.et[u % 2][:, i * P:(i + 1) * P],
                                            start=True, stop=True)
                last.then_inc(sem.av_done, 1)

            def attn_transpose(p, front):
                pe.wait_ge(sem.norm_done, 2 * p + 2)
                if front:
                    pe.wait_ge(sem.klo_done, p + 3)
                for k in range(KD):
                    last = nc.tensor.transpose(MB[:, k * P:(k + 1) * P],
                                               b.attn[:, k // 2, (k % 2) * P:(k % 2 + 1) * P], c.ident[:, :])
                last.then_inc(sem.attnT_done, 1)

            def out_project(p, front):
                pe.wait_ge(sem.alo_done, p + 1)
                if front:
                    pe.wait_ge(sem.qlo_done, p + 3)
                product(MA[:, :], three(lambda i, k: b.aT[i][:, k, :], lambda i, k: c.wo[i][:, k, :], KD), sem.o_done)

            ctx_transpose(0, 0, 0)
            k_project(0)
            x_transpose(0, False)
            k_transpose(0)
            q_project(0, False)
            v_project(0, False)
            ctx_transpose(1, 0, 1)
            q_transpose(0)
            scores(0, 0, 0, 0)

            def step(t, r, par):
                tail, own, front, ahead = stages(t)
                n, p = t + 1, t - 1
                if own:
                    scores(t, 1, r, par)
                    e_transpose(t, 0)
                if tail:
                    values(p, 7, 1 - par)
                if front:
                    k_project(n)
                if tail:
                    out_transpose(p, 0, own, front)
                if own:
                    e_transpose(t, 1)
                    values(t, 0, par)
                if front:
                    x_transpose(n, tail)
                if own:
                    scores(t, 2, r, par)
                if tail:
                    out_transpose(p, 1, own, front)
                if own:
                    e_transpose(t, 2)
                    values(t, 1, par)
                if front:
                    k_transpose(n)
                if own:
                    e_transpose(t, 3)
                    values(t, 2, par)
                if front:
                    q_project(n, tail)
                if own:
                    scores(t, 3, r, par)
                    e_transpose(t, 4)
                    values(t, 3, par)
                if tail:
                    attn_transpose(p, front)
                if own:
                    e_transpose(t, 5)
                    values(t, 4, par)
                if front:
                    q_transpose(n)
                    v_project(n, tail)
                if own:
                    e_transpose(t, 6)
                    values(t, 5, par)
                if front:
                    scores(n, 0, r + par, 1 - par)
                if own:
                    e_transpose(t, 7)
                    values(t, 6, par)
                if ahead:
                    ctx_transpose(n + 1, r + 1, par)
                if tail:
                    out_project(p, front)

            steps(step, pe)


def by_nibble(x):
    return x.rearrange("p (w j h) -> p w h j", j=4, h=2)


def ffn_weights(nc, sem, c, w, tmp, ps, A_gu, A_gus, A_dn, A_dns):
    halves = ((tmp.gu, 2 * INTER // P, DIM // 8, tmp.gu_val), (tmp.dn, DIM // P, INTER // 8, tmp.dn_val))
    units = [("gu", g, o, min(4, 2 * INTER // P - o)) for g in range(KD) for o in range(0, 2 * INTER // P, 4)]
    per_group = len(units) // KD
    units += [("dn", g, 0, KD) for g in range(KI)]

    def target(unit, i):
        kind, g, o, n = unit
        return by_nibble(w.gu[i][:, g, o * P:(o + n) * P]) if kind == "gu" else w.dn[i][:, g, :]

    def source(unit, i):
        cols = tmp.fw[i % 2][:, 0:unit[3] * P]
        return cols.rearrange("p (w h j) -> p w h j", h=2, j=4) if unit[0] == "gu" else cols

    def scale(unit):
        kind, g, o, n = unit
        return tmp.gu_scale[:, g % 2, o * P:(o + n) * P] if kind == "gu" else tmp.dn_scale[:, g, :]

    with nc.Block() as block:

        @block.sync
        def _(sp):
            sp.dma_start(tmp.gu[:, :, :], A_gu.rearrange("(t p) w -> p t w", p=P)).then_inc(sem.gu_loaded, 16)
            sp.dma_start(tmp.dn[:, :, :], A_dn.rearrange("(t p) w -> p t w", p=P)).then_inc(sem.dn_loaded, 16)

        @block.scalar
        def _(act):
            def load_scale(g):
                act.dma_start(tmp.gu_scale[:, g % 2, :], A_gus[g:g + 1, :].broadcast_to([P, 2 * INTER])).then_inc(
                    sem.gu_scale_loaded[g % 2], 16)

            load_scale(0)
            load_scale(1)
            act.dma_start(tmp.dn_scale[:, :, :], A_dns.rearrange("(a g) o -> a g o", a=1).broadcast_to(
                [P, KI, DIM])).then_inc(sem.dn_scale_loaded, 16)
            for i, unit in enumerate(units):
                act.wait_ge(sem.fw_done, i + 1)
                if (i + 1) % per_group == 0 and (i + 1) // per_group <= KD - 2:
                    load_scale((i + 1) // per_group + 1)
                act.activation(target(unit, 0), source(unit, i), ACT.Copy).then_inc(sem.fhi_done, 1)

        @block.gpsimd
        def _(pool):
            for i, unit in enumerate(units):
                pool.wait_ge(sem.fhi_done, i + 1)
                pool.tensor_tensor(target(unit, 1), source(unit, i), target(unit, 0).bitcast(F32),
                                   ALU.subtract).then_inc(sem.flo_done, 1)
            pool.wait_ge(sem.flo_done, len(units))

        @block.vector
        def _(dve):
            n = 0
            for (words, tiles, per_row, value), loaded in zip(halves, (sem.gu_loaded, sem.dn_loaded)):
                dve.wait_ge(loaded, 16)
                for j in range(4):
                    sgn = tmp.sgn[:, 0:tiles * per_row].rearrange("p (t w) -> p t w", t=tiles)
                    if n >= 1:
                        dve.wait_ge(sem.or_done, n)
                    up = 9 - 4 * j
                    dve.tensor_scalar(value[:, :, :, j], words[:, :, :], abs(up), 0x0E000E00,
                                      ALU.logical_shift_left if up >= 0 else ALU.logical_shift_right, ALU.bitwise_and)
                    dve.tensor_scalar(sgn, words[:, :, :], 12 - 4 * j, 0x80008000, ALU.logical_shift_left,
                                      ALU.bitwise_and).then_inc(sem.nibbles_done, 1)
                    dve.wait_ge(sem.nibbles_done, n + 1)
                    dve.tensor_tensor(value[:, :, :, j], value[:, :, :, j], sgn,
                                      ALU.bitwise_or).then_inc(sem.or_done, 1)
                    n += 1
            dve.wait_ge(sem.dn_scale_loaded, 16)
            for i, unit in enumerate(units):
                if unit[0] == "gu":
                    dve.wait_ge(sem.gu_scale_loaded[unit[1] % 2], 16 * (unit[1] // 2 + 1))
                dve.wait_ge(sem.fT_done, i + 1)
                if i >= 2:
                    dve.wait_ge(sem.flo_done, i - 1)
                cols = unit[3] * P
                dve.scalar_tensor_tensor(out=tmp.fw[i % 2][:, 0:cols], in0=ps[i % 2][:, :].bitcast(F16)[:, 0:cols],
                                         scalar=16384.0, in1=scale(unit), op0=ALU.mult,
                                         op1=ALU.mult).then_inc(sem.fw_done, 1)

        @block.tensor
        def _(pe):
            for i, (kind, g, o, n) in enumerate(units):
                value = tmp.gu_val if kind == "gu" else tmp.dn_val
                pe.wait_ge(sem.or_done, 4 if kind == "gu" else 8)
                if i >= 2:
                    pe.wait_ge(sem.fw_done, i - 1)
                for k in range(n):
                    rows = value[:, o + k, 16 * g:16 * g + 16, :].rearrange("p w j -> p (w j)").bitcast(F16)
                    last = nc.tensor.transpose(ps[i % 2][:, :].bitcast(F16)[:, k * P:(k + 1) * P], rows,
                                               c.ident16[:, :])
                last.then_inc(sem.fT_done, 1)


def ffn(nc, sem, c, w, b, ps, x1_dram, out, tiles):
    chunks = tiles // CHUNK

    def pairs_of(step, engine):
        step(0, 0, 0)
        step(1, 0, 1)
        with engine.Fori(1, chunks // 2 - 1) as r:
            step(2 * r, r, 0)
            step(2 * r + 1, r, 1)
        step(chunks - 2, chunks // 2 - 1, 0)
        step(chunks - 1, chunks // 2 - 1, 1)

    def more(m):
        return not isinstance(m, int) or m + 1 < chunks

    with nc.Block() as block:

        @block.sync
        def _(sp):
            def load(m, par):
                sp.dma_start(b.x[par][:, :, :], x1_dram[bass.ds(CHUNK * m, CHUNK), :, :].rearrange(
                    "t p n -> p t n")).then_inc(sem.f_loaded[par], 16)

            load(0, 0)

            def step(m, r, par):
                if more(m):
                    wait(sp, sem.f_stored[1 - par], 16 * CHUNK * (r + par))
                    load(m + 1, 1 - par)
                for j in range(CHUNK):
                    sp.wait_ge(sem.f_out_done, CHUNK * m + j + 1)
                    sp.dma_start(out[bass.ds(CHUNK * m + j, 1), :, :].rearrange("a p n -> p (a n)"),
                                 b.x[par][:, j, :]).then_inc(sem.f_stored[par], 16)

            pairs_of(step, sp)
            for par in range(2):
                sp.wait_ge(sem.f_stored[par], 16 * CHUNK * (chunks // 2))

        @block.gpsimd
        def _(pool):
            def rstd(m):
                pool.wait_ge(sem.f_stats_done, m + 1)
                pool.tensor_tensor(b.rstd[:, :], b.mv[:, :, 1], c.ln_eps[:, 0:1].broadcast_to([P, CHUNK]),
                                   ALU.add).then_inc(sem.f_vareps_done, 1)
                pool.wait_ge(sem.f_vareps_done, m + 1)
                pool.tensor_tensor(b.rstd[:, :], b.rstd[:, :], c.minus_half[:, 0:1].broadcast_to([P, CHUNK]),
                                   ALU.pow).then_inc(sem.f_rstd_done, 1)

            rstd(0)

            def step(m, r, par):
                for i in range(KI):
                    U = KI * m + i
                    pool.wait_ge(sem.hhi_done, U + 1)
                    pool.tensor_tensor(b.h[1][:, i, :], b.g[i % 3][:, :], b.h[0][:, i, :].bitcast(F32),
                                       ALU.subtract).then_inc(sem.hlo_done, 1)
                    if i == 5 and more(m):
                        rstd(m + 1)
                for j in range(CHUNK):
                    M = CHUNK * m + j
                    pool.wait_ge(sem.square_done, M + 1)
                    wait(pool, sem.f_out_done, M)
                    pool.tensor_tensor(b.rrms[:, :], b.ssq[:, j:j + 1], c.rms_eps[:, :], ALU.add).then_inc(sem.ms_done, 1)
                    pool.wait_ge(sem.ms_done, M + 1)
                    pool.tensor_tensor(b.rrms[:, :], b.rrms[:, :], c.minus_half[:, :], ALU.pow).then_inc(
                        sem.rrms_done, 1)

            pairs_of(step, pool)

        @block.scalar
        def _(act):
            def silu(m, i):
                U = KI * m + i
                act.wait_ge(sem.gate_done, U + 1)
                wait(act, sem.hlo_done, U - 1 if i < 2 else U - 2)
                act.activation(b.g[i % 3][:, :], ps.gate[i % 2][:, :], ACT.Silu).then_inc(sem.silu_done, 1)

            def h_hi(m, i):
                U = KI * m + i
                act.wait_ge(sem.mul_done, U + 1)
                act.activation(b.h[0][:, i, :], b.g[i % 3][:, :], ACT.Copy).then_inc(sem.hhi_done, 1)

            def z_hi(m, j):
                act.wait_ge(sem.zT_done, CHUNK * m + j + 1)
                act.activation(b.zT[0][:, :, j * P:(j + 1) * P], ps.z[j % 2][:, :].rearrange("p (k n) -> p k n", k=KD),
                               ACT.Copy).then_inc(sem.zhi_done, 1)

            for j in range(CHUNK):
                z_hi(0, j)

            def step(m, r, par):
                for i in range(KI + 1):
                    if i < KI:
                        silu(m, i)
                    if i >= 1:
                        h_hi(m, i - 1)
                if more(m):
                    for j in range(CHUNK):
                        z_hi(m + 1, j)
                for j in range(CHUNK):
                    act.wait_ge(sem.y_done, CHUNK * m + j + 1)
                    wait(act, sem.rrms_done, CHUNK * m + j - 1)
                    act.activation(b.junk[j % 2][:, :], ps.y[j % 2][:, :], ACT.Square, scale=DIM ** -0.5,
                                   accum_out=b.ssq[:, j:j + 1]).then_inc(sem.square_done, 1)

            pairs_of(step, act)

        @block.vector
        def _(dve):
            def stats(m, r, par):
                dve.wait_ge(sem.f_loaded[par], 16 * (r + 1))
                for j in range(CHUNK):
                    last = dve.bn_stats(b.bn[:, j, :], b.x[par][:, j, :])
                last.then_inc(sem.f_bn_done, 1)

            def mean_variance():
                for j in range(CHUNK):
                    last = dve.bn_aggr(b.mv[:, j, :], b.bn[:, j, :])
                last.then_inc(sem.f_stats_done, 1)

            def normalise(m, par, j):
                if j == 0:
                    dve.wait_ge(sem.f_rstd_done, m + 1)
                wait(dve, sem.zT_done, CHUNK * m + j - 1)
                dve.tensor_scalar(by_nibble(b.z[j % 2][:, :]),
                                  b.x[par][:, j, :].rearrange("p (w h j) -> p w h j", h=2, j=4),
                                  b.mv[:, j, 0:1], b.rstd[:, j:j + 1], ALU.subtract, ALU.mult).then_inc(sem.z_done, 1)

            def z_lo(m, j):
                dve.wait_ge(sem.zhi_done, CHUNK * m + j + 1)
                dve.tensor_tensor(b.zT[1][:, :, j * P:(j + 1) * P],
                                  ps.z[j % 2][:, :].rearrange("p (k n) -> p k n", k=KD),
                                  b.zT[0][:, :, j * P:(j + 1) * P].bitcast(F32), ALU.subtract).then_inc(sem.zlo_done, 1)

            stats(0, 0, 0)
            dve.wait_ge(sem.f_bn_done, 1)
            mean_variance()
            normalise(0, 0, 0)
            normalise(0, 0, 1)
            for j in range(CHUNK):
                z_lo(0, j)
                if j < 2:
                    normalise(0, 0, j + 2)

            def step(m, r, par):
                for i in range(KI):
                    U = KI * m + i
                    dve.wait_ge(sem.up_done, U + 1)
                    dve.wait_ge(sem.silu_done, U + 1)
                    if i == 5 and more(m):
                        dve.wait_ge(sem.f_bn_done, m + 2)
                    dve.tensor_tensor(b.g[i % 3][:, :], b.g[i % 3][:, :], ps.up[i % 2][:, :],
                                      ALU.mult).then_inc(sem.mul_done, 1)
                    if more(m):
                        if i == 4:
                            stats(m + 1, r + par, 1 - par)
                        if i == 5:
                            mean_variance()
                        if i in (7, 9):
                            normalise(m + 1, 1 - par, (i - 7) // 2)
                if more(m):
                    for j in range(CHUNK):
                        z_lo(m + 1, j)
                        if j < 2:
                            normalise(m + 1, 1 - par, j + 2)
                for j in range(CHUNK):
                    dve.wait_ge(sem.rrms_done, CHUNK * m + j + 1)
                    dve.scalar_tensor_tensor(out=b.x[par][:, j, :], in0=ps.y[j % 2][:, :], scalar=b.rrms[:, 0:1],
                                             in1=b.x[par][:, j, :], op0=ALU.mult, op1=ALU.add).then_inc(
                                                 sem.f_out_done, 1)

            pairs_of(step, dve)

        @block.tensor
        def _(pe):
            passes = ((0, 1), (1, 0), (0, 0))

            def z_transpose(m):
                for j in range(CHUNK):
                    M = CHUNK * m + j
                    pe.wait_ge(sem.z_done, M + 1)
                    wait(pe, sem.zlo_done, M - 1)
                    for k in range(KD):
                        last = nc.tensor.transpose(ps.z[j % 2][:, k * P:(k + 1) * P],
                                                   b.z[j % 2][:, k * P:(k + 1) * P], c.ident[:, :])
                    last.then_inc(sem.zT_done, 1)

            def gate_up(m):
                pe.wait_ge(sem.zlo_done, CHUNK * m + CHUNK)
                for i in range(KI):
                    U = KI * m + i
                    for bank, read, column, done in ((ps.gate[i % 2], sem.silu_done, i * P, sem.gate_done),
                                                     (ps.up[i % 2], sem.mul_done, INTER + i * P, sem.up_done)):
                        wait(pe, read, U if i == 0 else U - 1)
                        n = 0
                        for a, x in passes:
                            for k in range(KD):
                                last = nc.tensor.matmul(bank[:, :], w.gu[a][:, k, column:column + P],
                                                        b.zT[x][:, k, :], start=(n == 0), stop=(n == 3 * KD - 1))
                                n += 1
                        last.then_inc(done, 1)

            def down(m):
                for j in range(CHUNK):
                    M = CHUNK * m + j
                    wait(pe, sem.f_out_done, M - 1)
                    n = 0
                    for k in range(KI):
                        if j == 0:
                            pe.wait_ge(sem.hlo_done, KI * m + k + 1)
                        for a, x in passes:
                            last = nc.tensor.matmul(ps.y[j % 2][:, :], b.h[a][:, k, j * P:(j + 1) * P],
                                                    w.dn[x][:, k, :], start=(n == 0), stop=(n == 3 * KI - 1))
                            n += 1
                    last.then_inc(sem.y_done, 1)

            z_transpose(0)

            def step(m):
                gate_up(m)
                if more(m):
                    z_transpose(m + 1)
                down(m)

            step(0)
            with pe.Fori(1, chunks - 1) as m:
                step(m)
            step(chunks - 1)


def program(nc, A_x, A_ctx, A_pos, A_wq, A_wkv, A_wo, A_bout, A_gu, A_gus, A_dn, A_dns, out):
    tiles = A_x.shape[0]
    x1_dram = nc.dram_tensor("x1_scratch", [tiles, P, DIM], F32, kind="Internal").ap()

    with ExitStack() as whole:
        def semaphore(name):
            return whole.enter_context(nc.semaphore(name))

        def semaphores(name):
            return [semaphore(f"{name}{i}") for i in range(2)]

        sem = Named()
        sem.pos_loaded = semaphore("pos_loaded")
        sem.wq_loaded = semaphore("wq_loaded")
        sem.wkv_loaded = semaphore("wkv_loaded")
        sem.wo_loaded = semaphore("wo_loaded")
        sem.bout_loaded = semaphore("bout_loaded")
        sem.const_set = semaphore("const_set")
        sem.w_hi = semaphore("w_hi")
        sem.w_lo = semaphore("w_lo")
        sem.angles = semaphore("angles")
        sem.tables = semaphore("tables")
        sem.setup_chain = semaphore("setup_chain")
        sem.kblk_zeroed = semaphore("kblk_zeroed")
        sem.v_zeroed = semaphore("v_zeroed")
        sem.v_ones = semaphore("v_ones")
        sem.klo_done = semaphore("klo_done")
        sem.khi_done = semaphore("khi_done")
        sem.s_done = semaphore("s_done")
        sem.xb_done = semaphore("xb_done")
        sem.ctxT_done = semaphore("ctxT_done")
        sem.x1_done = semaphore("x1_done")
        sem.stats_done = semaphore("stats_done")
        sem.vareps_done = semaphore("vareps_done")
        sem.rstd_done = semaphore("rstd_done")
        sem.kmul_done = semaphore("kmul_done")
        sem.qmul_done = semaphore("qmul_done")
        sem.kT_done = semaphore("kT_done")
        sem.qT_done = semaphore("qT_done")
        sem.kr_done = semaphore("kr_done")
        sem.qr_done = semaphore("qr_done")
        sem.v_done = semaphore("v_done")
        sem.q_done = semaphore("q_done")
        sem.k_done = semaphore("k_done")
        sem.xT_done = semaphore("xT_done")
        sem.chi_done = semaphore("chi_done")
        sem.xhi_done = semaphore("xhi_done")
        sem.qhi_done = semaphore("qhi_done")
        sem.qlo_done = semaphore("qlo_done")
        sem.v_copied = semaphore("v_copied")
        sem.sub_done = semaphore("sub_done")
        sem.exp_done = semaphore("exp_done")
        sem.et_done = semaphore("et_done")
        sem.et_copied = semaphore("et_copied")
        sem.av_done = semaphore("av_done")
        sem.av_copied = semaphore("av_copied")
        sem.outT_done = semaphore("outT_done")
        sem.attnT_done = semaphore("attnT_done")
        sem.ahi_done = semaphore("ahi_done")
        sem.alo_done = semaphore("alo_done")
        sem.o_done = semaphore("o_done")
        sem.bn_done = semaphore("bn_done")
        sem.xn_done = semaphore("xn_done")
        sem.clo_done = semaphore("clo_done")
        sem.xlo_done = semaphore("xlo_done")
        sem.mx_done = semaphore("mx_done")
        sem.rsum_done = semaphore("rsum_done")
        sem.norm_done = semaphore("norm_done")
        sem.gu_loaded = semaphore("gu_loaded")
        sem.dn_loaded = semaphore("dn_loaded")
        sem.dn_scale_loaded = semaphore("dn_scale_loaded")
        sem.fw_done = semaphore("fw_done")
        sem.fhi_done = semaphore("fhi_done")
        sem.flo_done = semaphore("flo_done")
        sem.nibbles_done = semaphore("nibbles_done")
        sem.or_done = semaphore("or_done")
        sem.fT_done = semaphore("fT_done")
        sem.f_out_done = semaphore("f_out_done")
        sem.f_stats_done = semaphore("f_stats_done")
        sem.f_vareps_done = semaphore("f_vareps_done")
        sem.f_rstd_done = semaphore("f_rstd_done")
        sem.f_bn_done = semaphore("f_bn_done")
        sem.hhi_done = semaphore("hhi_done")
        sem.hlo_done = semaphore("hlo_done")
        sem.square_done = semaphore("square_done")
        sem.ms_done = semaphore("ms_done")
        sem.rrms_done = semaphore("rrms_done")
        sem.gate_done = semaphore("gate_done")
        sem.up_done = semaphore("up_done")
        sem.silu_done = semaphore("silu_done")
        sem.mul_done = semaphore("mul_done")
        sem.zT_done = semaphore("zT_done")
        sem.zhi_done = semaphore("zhi_done")
        sem.zlo_done = semaphore("zlo_done")
        sem.z_done = semaphore("z_done")
        sem.y_done = semaphore("y_done")
        sem.x_loaded = semaphores("x_loaded")
        sem.ctx_loaded = semaphores("ctx_loaded")
        sem.kblk_ready = semaphores("kblk_ready")
        sem.x1_stored = semaphores("x1_stored")
        sem.f_loaded = semaphores("f_loaded")
        sem.f_stored = semaphores("f_stored")
        sem.gu_scale_loaded = semaphores("gu_scale_loaded")

        def sbuf(stack, name, shape, dt=F32):
            return stack.enter_context(nc.sbuf_tensor(name, shape, dt))

        def psum(stack, name, columns):
            return stack.enter_context(nc.psum_tensor(name, [P, columns], F32))

        c = Named()
        c.ident = sbuf(whole, "ident", [P, P])
        c.ident16 = sbuf(whole, "ident16", [P, P], F16)
        c.minus_half = sbuf(whole, "minus_half", [P, 1])
        c.ln_eps = sbuf(whole, "ln_eps", [P, 1])
        c.rms_eps = sbuf(whole, "rms_eps", [P, 1])

        with ExitStack() as phase:
            c.bout = sbuf(phase, "bout", [P, DIM])
            c.cos = sbuf(phase, "cos", [P, tiles, 2, HD // 2])
            c.sin = sbuf(phase, "sin", [P, tiles, 2, HD // 2])
            c.wq = [sbuf(phase, f"wq{i}", [P, KD, DIM], F32R) for i in range(2)]
            c.wkv = [sbuf(phase, f"wkv{i}", [P, KC, 2 * DIM], F32R) for i in range(2)]
            c.wo = [sbuf(phase, f"wo{i}", [P, KD, DIM], F32R) for i in range(2)]
            with ExitStack() as scratch:
                tmp = Named()
                tmp.pos = sbuf(scratch, "pos", [P, tiles, 2])
                tmp.ang = sbuf(scratch, "ang", [P, tiles, HD // 2])
                tmp.turns = sbuf(scratch, "turns", [P, tiles, HD // 2])
                tmp.ang_s = sbuf(scratch, "ang_s", [P, tiles, HD // 2])
                tmp.ang_c = sbuf(scratch, "ang_c", [P, tiles, HD // 2])
                tmp.wq = sbuf(scratch, "wq_raw", [P, KD, DIM])
                tmp.wkv = sbuf(scratch, "wkv_raw", [P, KC, 2 * DIM])
                tmp.wo = sbuf(scratch, "wo_raw", [P, KD, DIM])
                setup_constants(nc, sem, c, tmp, A_pos, A_wq, A_wkv, A_wo, A_bout, tiles)

            b = Named()
            b.x = [sbuf(phase, f"x{i}", [P, DIM]) for i in range(2)]
            b.ctx = [sbuf(phase, f"ctx{i}", [P, CTX]) for i in range(2)]
            b.xb = [sbuf(phase, f"xb{i}", [P, DIM]) for i in range(2)]
            b.x1 = [sbuf(phase, f"x1_{i}", [P, DIM]) for i in range(2)]
            b.bn = sbuf(phase, "bn", [P, 6])
            b.mv = sbuf(phase, "mv", [P, 2])
            b.rstd = sbuf(phase, "rstd", [P, 1])
            b.xn = sbuf(phase, "xn", [P, DIM])
            b.xT = [sbuf(phase, f"xT{i}", [P, KD, P], F32R) for i in range(2)]
            b.cT = [sbuf(phase, f"cT{i}", [P, KC, P], F32R) for i in range(2)]
            b.rope = [[sbuf(phase, f"rope{w}{i}", [P, DIM]) for i in range(2)] for w in "kq"]
            b.kr = sbuf(phase, "kr", [P, DIM])
            b.qr = sbuf(phase, "qr", [P, DIM])
            b.kT = sbuf(phase, "kT", [P, 2, KD, P], F32R)
            b.kblk = [sbuf(phase, f"kblk{i}", [P, 2, KD, HPT, P], F32R) for i in range(2)]
            b.qT = [[sbuf(phase, f"qT{i}{j}", [P, KD, P], F32R) for j in range(2)] for i in range(2)]
            b.v = [sbuf(phase, f"v{i}", [P, HEADS, 2 * HD]) for i in range(2)]
            b.mx = [sbuf(phase, f"mx{i}", [P, HPT]) for i in range(2)]
            b.e = [sbuf(phase, f"e{i}", [P, HPT * P]) for i in range(2)]
            b.et = [sbuf(phase, f"et{i}", [P, 4 * P]) for i in range(2)]
            b.avT = [sbuf(phase, f"avT{i}", [P, 4 * P]) for i in range(2)]
            b.rsum = [sbuf(phase, f"rsum{i}", [P, HEADS // 2]) for i in range(2)]
            b.attn = sbuf(phase, "attn", [P, 2, DIM // 2])
            b.aT = [sbuf(phase, f"aT{i}", [P, KD, P], F32R) for i in range(2)]
            ps = Named()
            ps.scores = [psum(phase, f"scores{i}", 1024) for i in range(2)]
            ps.et = psum(phase, "et_ps", 512)
            ps.av = psum(phase, "av_ps", 512)
            ps.misc_a = psum(phase, "misc_a", 512)
            ps.misc_b = psum(phase, "misc_b", 512)
            attention(nc, sem, c, b, ps, A_x, A_ctx, x1_dram, tiles)

        w = Named()
        w.gu = [sbuf(whole, f"w_gu{i}", [P, KD, 2 * INTER], F32R) for i in range(2)]
        w.dn = [sbuf(whole, f"w_dn{i}", [P, KI, DIM], F32R) for i in range(2)]
        with ExitStack() as scratch:
            tmp = Named()
            tmp.gu = sbuf(scratch, "gu_packed", [P, 2 * INTER // P, DIM // 8], U32)
            tmp.dn = sbuf(scratch, "dn_packed", [P, KD, INTER // 8], U32)
            tmp.gu_val = sbuf(scratch, "gu_val", [P, 2 * INTER // P, DIM // 8, 4], U32)
            tmp.dn_val = sbuf(scratch, "dn_val", [P, KD, INTER // 8, 4], U32)
            tmp.sgn = sbuf(scratch, "sgn", [P, 2 * INTER // P * DIM // 8], U32)
            tmp.gu_scale = sbuf(scratch, "gu_scale", [P, 2, 2 * INTER], F16)
            tmp.dn_scale = sbuf(scratch, "dn_scale", [P, KI, DIM], F16)
            tmp.fw = [sbuf(scratch, f"fw{i}", [P, 512]) for i in range(2)]
            ps = [psum(scratch, f"fT{i}", 512) for i in range(2)]
            ffn_weights(nc, sem, c, w, tmp, ps, A_gu, A_gus, A_dn, A_dns)

        b = Named()
        b.x = [sbuf(whole, f"fx{i}", [P, CHUNK, DIM]) for i in range(2)]
        b.z = [sbuf(whole, f"z{i}", [P, DIM]) for i in range(2)]
        b.zT = [sbuf(whole, f"zT{i}", [P, KD, CHUNK * P], F32R) for i in range(2)]
        b.g = [sbuf(whole, f"g{i}", [P, CHUNK * P]) for i in range(3)]
        b.h = [sbuf(whole, f"h{i}", [P, KI, CHUNK * P], F32R) for i in range(2)]
        b.junk = [sbuf(whole, f"junk{i}", [P, DIM], F16) for i in range(2)]
        b.bn = sbuf(whole, "fbn", [P, CHUNK, 6])
        b.mv = sbuf(whole, "fmv", [P, CHUNK, 2])
        b.rstd = sbuf(whole, "frstd", [P, CHUNK])
        b.ssq = sbuf(whole, "ssq", [P, CHUNK])
        b.rrms = sbuf(whole, "rrms", [P, 1])
        ps = Named()
        ps.gate = [psum(whole, f"gate{i}", 512) for i in range(2)]
        ps.up = [psum(whole, f"up{i}", 512) for i in range(2)]
        ps.z = [psum(whole, f"z_ps{i}", 512) for i in range(2)]
        ps.y = [psum(whole, f"y_ps{i}", 512) for i in range(2)]
        ffn(nc, sem, c, w, b, ps, x1_dram, out, tiles)


INPUTS = ["x", "ctx_1024", "fside_BxSx2_0", "L0_xattn_Wq", "L0_xattn_Wkv", "L0_xattn_Wout", "L0_xattn_bout",
          "L0_ffn_gate_up_packed", "L0_ffn_gate_up_scales", "L0_ffn_down_packed", "L0_ffn_down_scales"]


def kernel(**inputs):
    import numpy as np
    import concourse.bacc as bacc
    from concourse.bass_utils import run_bass_kernel_spmd

    nc = bacc.Bacc("TRN2", target_bir_lowering=False, num_devices=1, dynamic_dma_scratch_size=1024)
    arrays, args = {}, []
    for name in INPUTS:
        a = np.ascontiguousarray(inputs[name])
        if a.dtype == np.int32:
            a = a.view(np.uint32)
        arrays[f"in_{name}"] = a
        args.append(nc.dram_tensor(f"in_{name}", a.shape, mybir.dt.from_np(a.dtype), kind="ExternalInput").ap())
    out = nc.dram_tensor("out", inputs["x"].shape, F32, kind="ExternalOutput").ap()
    program(nc, *args, out)
    result = run_bass_kernel_spmd(nc, [arrays], core_ids=[0])
    return result.results[0]["out"]
```

```python
import concourse.bass as bass
from concourse import mybir
from contextlib import ExitStack

F32 = mybir.dt.float32
F32R = mybir.dt.float32r
F16 = mybir.dt.float16
U32 = mybir.dt.uint32
ALU = mybir.AluOpType
ACT = mybir.ActivationFunctionType
AX = mybir.AxisListType

P = 128
DIM = 512
CTX = 256
HEADS = 32
HD = DIM // HEADS
INTER = 1408
GROUP = 128
KD = DIM // P
KC = CTX // P
KI = INTER // P
HPT = P // HD
UNITS = HEADS // 4
LN_EPS = 1e-5
RMS_EPS = 1e-6
CHUNK = 4

TWO_PI = 6.283185307179586
PI_A = 6.28125
PI_B = 0.0019340515136718750
PI_C = TWO_PI - PI_A - PI_B
ROUND = 12582912.0
PI_IN = 3.1415925


class Named:
    pass


def wait(engine, semaphore, value):
    if not isinstance(value, int) or value > 0:
        engine.wait_ge(semaphore, value)


def setup_constants(nc, sem, c, b, tmp, A_pos, A_wq, A_wkv, A_wo, A_bout, A_gu, A_dn, tiles):
    with nc.Block() as block:

        @block.sync
        def _(sp):
            sp.dma_start(tmp.pos[:, :, :], A_pos.rearrange("t p a -> p t a")).then_inc(sem.pos_loaded, 16)
            sp.dma_start(tmp.wq[:, :, :], A_wq.rearrange("(k p) n -> p k n", p=P)).then_inc(sem.wq_loaded, 16)
            sp.dma_start(tmp.wkv[:, :, :], A_wkv.rearrange("(k p) n -> p k n", p=P)).then_inc(sem.wkv_loaded, 16)
            sp.dma_start(tmp.wo[:, :, :], A_wo.rearrange("(k p) n -> p k n", p=P)).then_inc(sem.wo_loaded, 16)
            sp.dma_start(c.bout[:, :], A_bout.rearrange("(a n) -> a n", a=1).broadcast_to([P, DIM])).then_inc(
                sem.bout_loaded, 16)
            sp.dma_start(c.gu_packed[:, :, :], A_gu.rearrange("(t p) w -> p t w", p=P)).then_inc(sem.gu_loaded, 16)
            sp.dma_start(c.dn_packed[:, :, :], A_dn.rearrange("(t p) w -> p t w", p=P)).then_inc(sem.dn_loaded, 16)
            sp.wait_ge(sem.bout_loaded, 16)
            sp.wait_ge(sem.gu_loaded, 16)
            sp.wait_ge(sem.dn_loaded, 16)

        @block.gpsimd
        def _(pool):
            pool.memset(c.ident[:, :], 0.0).then_inc(sem.const_set, 1)
            pool.memset(c.ident16[:, :], 0.0).then_inc(sem.const_set, 1)
            pool.memset(c.minus_half[:, :], -0.5).then_inc(sem.const_set, 1)
            pool.memset(c.ln_eps[:, :], LN_EPS).then_inc(sem.const_set, 1)
            pool.memset(c.rms_eps[:, :], RMS_EPS).then_inc(sem.const_set, 1)
            pool.wait_ge(sem.const_set, 5)
            for ident in (c.ident, c.ident16):
                pool.affine_select(out=ident[:, :], in_=ident[:, :], compare_op=ALU.not_equal, fill=1.0, base=0,
                                   pattern=[[-1, P]], channel_multiplier=1).then_inc(sem.const_set, 1)
            for v in b.v:
                pool.memset(v[:, :, :], 0.0).then_inc(sem.v_zeroed, 1)
            pool.wait_ge(sem.v_zeroed, 2)
            for v in b.v:
                pool.memset(v[:, :, HD:HD + 1], 1.0).then_inc(sem.v_ones, 1)
            for kblk in b.kblk:
                pool.memset(kblk[:, :, :, :, :].rearrange("p j a k n -> p (j a k n)").bitcast(U32),
                            0).then_inc(sem.kblk_zeroed, 1)
            pool.wait_ge(sem.const_set, 7)
            pool.wait_ge(sem.v_ones, 2)
            pool.wait_ge(sem.kblk_zeroed, 2)

        def permuted(w):
            return w.rearrange("p k (h i e) -> p k h e i", e=2, i=HD // 2)

        def plain(w):
            return w.rearrange("p k (h e i) -> p k h e i", e=2, i=HD // 2)

        def parts():
            for k in range(KD):
                yield sem.wq_loaded, tmp.wq[:, k:k + 1, :], (c.wq[0][:, k:k + 1, :], c.wq[1][:, k:k + 1, :]), True
            for k in range(KC):
                yield (sem.wkv_loaded, tmp.wkv[:, k:k + 1, 0:DIM],
                       (c.wkv[0][:, k:k + 1, 0:DIM], c.wkv[1][:, k:k + 1, 0:DIM]), True)
                yield (sem.wkv_loaded, tmp.wkv[:, k:k + 1, DIM:2 * DIM],
                       (c.wkv[0][:, k:k + 1, DIM:2 * DIM], c.wkv[1][:, k:k + 1, DIM:2 * DIM]), False)
            for k in range(KD):
                yield sem.wo_loaded, tmp.wo[:, k:k + 1, :], (c.wo[0][:, k:k + 1, :], c.wo[1][:, k:k + 1, :]), False

        @block.scalar
        def _(act):
            for loaded, src, (hi, _), permute in parts():
                act.wait_ge(loaded, 16)
                s, d = (permuted(src), plain(hi)) if permute else (src, hi)
                act.activation(d[:, 0], s[:, 0], ACT.Copy).then_inc(sem.w_hi, 1)
            act.wait_ge(sem.angles, 1)
            act.activation(c.sin[:, :, 0, :], tmp.ang_s[:, :, :], ACT.Sin, scale=-1.0)
            act.activation(c.sin[:, :, 1, :], tmp.ang_s[:, :, :], ACT.Sin)
            act.activation(c.cos[:, :, 0, :], tmp.ang_c[:, :, :], ACT.Sin)
            act.activation(c.cos[:, :, 1, :], tmp.ang_c[:, :, :], ACT.Sin).then_inc(sem.tables, 1)
            act.wait_ge(sem.tables, 1)

        @block.vector
        def _(dve):
            steps = [0]

            def then(ins):
                steps[0] += 1
                ins.then_inc(sem.setup_chain, 1)
                dve.wait_ge(sem.setup_chain, steps[0])

            dve.wait_ge(sem.pos_loaded, 16)
            ang, n, r = tmp.ang, tmp.turns, (tmp.ang_s, tmp.ang_c)
            for f in range(4):
                last = dve.tensor_scalar(ang[:, :, :].rearrange("p t (a f) -> p t a f", f=4)[:, :, :, f],
                                         tmp.pos[:, :, :], float(10000.0 ** (-f / 4.0)), None, ALU.mult)
            then(last)
            for i, (quarter, shift) in enumerate(((0.0, 0.0), (0.25, TWO_PI / 4))):
                then(dve.tensor_scalar(n[:, :, :], ang[:, :, :], 1 / TWO_PI, quarter, ALU.mult, ALU.add))
                then(dve.tensor_scalar(n[:, :, :], n[:, :, :], ROUND, ROUND, ALU.add, ALU.subtract))
                src = ang
                for part in (PI_A, PI_B, PI_C):
                    then(dve.scalar_tensor_tensor(out=r[i][:, :, :], in0=n[:, :, :], scalar=-part,
                                                  in1=src[:, :, :], op0=ALU.mult, op1=ALU.add))
                    src = r[i]
                then(dve.tensor_scalar(r[i][:, :, :], r[i][:, :, :], shift, PI_IN, ALU.add, ALU.min))
                then(dve.tensor_scalar(r[i][:, :, :], r[i][:, :, :], -PI_IN, None, ALU.max))
            dve.sem_inc(sem.angles, 1)
            for n_part, (loaded, src, (hi, lo), permute) in enumerate(parts()):
                dve.wait_ge(loaded, 16)
                dve.wait_ge(sem.w_hi, n_part + 1)
                s, h, d = ((permuted(src), plain(hi.bitcast(F32)), plain(lo)) if permute
                           else (src, hi.bitcast(F32), lo))
                dve.tensor_tensor(d[:, 0], s[:, 0], h[:, 0], ALU.subtract).then_inc(sem.w_lo, 1)


def unpack_nibbles(dve, sem, words, value, signs, j, n):
    wait(dve, sem.or_done, n)
    up = 9 - 4 * j
    dve.tensor_scalar(value[:, :, :, j], words[:, :, :], abs(up), 0x0E000E00,
                      ALU.logical_shift_left if up >= 0 else ALU.logical_shift_right, ALU.bitwise_and)
    dve.tensor_scalar(signs[:, :, :], words[:, :, :], 12 - 4 * j, 0x80008000, ALU.logical_shift_left,
                      ALU.bitwise_and).then_inc(sem.nibbles_done, 1)
    dve.wait_ge(sem.nibbles_done, n + 1)
    dve.tensor_tensor(value[:, :, :, j], value[:, :, :, j], signs[:, :, :], ALU.bitwise_or).then_inc(sem.or_done, 1)


def attention(nc, sem, c, b, ps, A_x, A_ctx, x1_dram, tiles):
    S, ET, AV, MA, MB = ps.scores, ps.et, ps.av, ps.misc_a, ps.misc_b

    def steps(step, engine):
        for t in range(4):
            step(t, t // 2, t % 2)
        with engine.Fori(2, tiles // 2 - 1) as r:
            step(2 * r, r, 0)
            step(2 * r + 1, r, 1)
        step(tiles - 2, tiles // 2 - 1, 0)
        step(tiles - 1, tiles // 2 - 1, 1)
        step(tiles, tiles // 2, 0)

    def stages(t):
        if isinstance(t, int):
            return t >= 1, t < tiles, t + 1 < tiles, t + 2 < tiles
        return True, True, True, True

    with nc.Block() as block:

        @block.sync
        def _(sp):
            def load_x(m, r, par):
                sp.dma_start(b.x[par][:, :], A_x[bass.ds(m, 1), :, :].rearrange("a p n -> p (a n)")).then_inc(
                    sem.x_loaded[par], 16)

            def load_ctx(m, r, par):
                sp.dma_start(b.ctx[par][:, :], A_ctx[bass.ds(m, 1), :, :].rearrange("a p n -> p (a n)")).then_inc(
                    sem.ctx_loaded[par], 16)

            def spread_k(n, r, par):
                sp.wait_ge(sem.klo_done, n + 1)
                wait(sp, sem.s_done, 4 * n - 4)
                for j in range(HPT):
                    rows = slice(HD * j, HD * (j + 1))
                    sp.dma_start(b.kblk[par][rows, j, :, :, :].bitcast(F32),
                                 b.kT[rows, :, :, :].bitcast(F32)).then_inc(sem.kblk_ready[par], 16)

            load_x(0, 0, 0)
            load_ctx(0, 0, 0)
            load_x(1, 0, 1)
            load_ctx(1, 0, 1)
            spread_k(0, 0, 0)

            def step(t, r, par):
                tail, own, front, ahead = stages(t)
                if ahead:
                    sp.wait_ge(sem.ctxT_done, t + 1)
                    load_ctx(t + 2, r + 1, par)
                    sp.wait_ge(sem.xb_done, t + 1)
                    load_x(t + 2, r + 1, par)
                if front:
                    spread_k(t + 1, r + par, 1 - par)
                if tail:
                    sp.wait_ge(sem.x1_done, t)
                    sp.dma_start(x1_dram[bass.ds(t - 1, 1), :, :].rearrange("a p n -> p (a n)"),
                                 b.x1[1 - par][:, :]).then_inc(sem.x1_stored[1 - par], 16)

            steps(step, sp)
            for par in range(2):
                sp.wait_ge(sem.x1_stored[par], 16 * (tiles // 2))

        @block.gpsimd
        def _(pool):
            def rstd(m):
                pool.wait_ge(sem.stats_done, m + 1)
                pool.tensor_tensor(b.rstd[:, :], b.mv[:, 1:2], c.ln_eps[:, :], ALU.add).then_inc(sem.vareps_done, 1)
                pool.wait_ge(sem.vareps_done, m + 1)
                pool.tensor_tensor(b.rstd[:, :], b.rstd[:, :], c.minus_half[:, :], ALU.pow).then_inc(sem.rstd_done, 1)

            def rope_add(n, which, products_done, rotated, transposed_done, added):
                pool.wait_ge(products_done, n + 1)
                wait(pool, transposed_done, n)
                pool.tensor_tensor(rotated[:, :], b.rope[which][0][:, :], b.rope[which][1][:, :],
                                   ALU.add).then_inc(added, 1)

            def rope_add_k(n):
                rope_add(n, 0, sem.kmul_done, b.kr, sem.kT_done, sem.kr_done)

            def rope_add_q(n):
                rope_add(n, 1, sem.qmul_done, b.qr, sem.qT_done, sem.qr_done)

            rstd(0)
            rope_add_k(0)
            rstd(1)
            rope_add_q(0)

            def step(t, r, par):
                tail, own, front, ahead = stages(t)
                if own:
                    wait(pool, sem.x1_done, t - 1)
                    pool.wait_ge(sem.x_loaded[par], 16 * (r + 1))
                    pool.tensor_tensor(b.xb[par][:, :], b.x[par][:, :], c.bout[:, :], ALU.add).then_inc(sem.xb_done, 1)
                if front:
                    rope_add_k(t + 1)
                    rope_add_q(t + 1)
                if ahead:
                    rstd(t + 2)

            steps(step, pool)

        @block.scalar
        def _(act):
            def ctx_hi(n):
                act.wait_ge(sem.ctxT_done, n + 1)
                wait(act, sem.v_done, n)
                act.activation(b.cT[0][:, :, :], MB[:, 0:CTX].rearrange("p (k n) -> p k n", k=KC),
                               ACT.Copy).then_inc(sem.chi_done, 1)

            def x_hi(n):
                act.wait_ge(sem.xT_done, n + 1)
                wait(act, sem.q_done, n)
                act.activation(b.xT[0][:, :, :], MB[:, :].rearrange("p (k n) -> p k n", k=KD),
                               ACT.Copy).then_inc(sem.xhi_done, 1)

            def k_hi(n, r, par):
                act.wait_ge(sem.kT_done, n + 1)
                wait(act, sem.kblk_ready[1 - par], 16 * HPT * (r + par))
                act.activation(b.kT[:, 0, :, :], MB[:, :].rearrange("p (k n) -> p k n", k=KD),
                               ACT.Copy).then_inc(sem.khi_done, 1)

            def q_hi(n, par):
                act.wait_ge(sem.qT_done, n + 1)
                wait(act, sem.s_done, 4 * n - 4)
                act.activation(b.qT[par][0][:, :, :], MA[:, :].rearrange("p (k n) -> p k n", k=KD),
                               ACT.Copy).then_inc(sem.qhi_done, 1)

            def v_copy(n, par):
                act.wait_ge(sem.v_done, n + 1)
                wait(act, sem.av_done, UNITS * (n - 1))
                act.activation(b.v[par][:, :, 0:HD], MB[:, :].rearrange("p (h d) -> p h d", d=HD),
                               ACT.Copy).then_inc(sem.v_copied, 1)

            def exps(t, g):
                G = 4 * t + g
                act.wait_ge(sem.sub_done, G + 1)
                act.activation(b.e[g % 2][:, :], b.e[g % 2][:, :], ACT.Exp, scale=HD ** -0.5).then_inc(sem.exp_done, 1)

            def et_copy(t, u):
                U = UNITS * t + u
                act.wait_ge(sem.et_done, U + 1)
                wait(act, sem.av_done, U - 1)
                act.activation(b.et[u % 2][:, :], ET[:, :], ACT.Copy).then_inc(sem.et_copied, 1)

            def av_copy(t, half):
                H = 2 * t + half
                act.wait_ge(sem.av_done, 4 * H + 4)
                wait(act, sem.outT_done, H - 1)
                act.activation(b.avT[half][:, :], AV[:, :], ACT.Copy).then_inc(sem.av_copied, 1)

            def attn_hi(p):
                act.wait_ge(sem.attnT_done, p + 1)
                wait(act, sem.o_done, p)
                act.activation(b.aT[0][:, :, :], MB[:, :].rearrange("p (k n) -> p k n", k=KD),
                               ACT.Copy).then_inc(sem.ahi_done, 1)

            ctx_hi(0)
            x_hi(0)
            k_hi(0, 0, 0)
            v_copy(0, 0)
            ctx_hi(1)
            q_hi(0, 0)
            exps(0, 0)

            def step(t, r, par):
                tail, own, front, ahead = stages(t)
                n, p = t + 1, t - 1
                if tail:
                    av_copy(p, 1)
                if own:
                    et_copy(t, 0)
                    exps(t, 1)
                if front:
                    x_hi(n)
                if own:
                    et_copy(t, 1)
                    et_copy(t, 2)
                if front:
                    k_hi(n, r + par, 1 - par)
                if own:
                    exps(t, 2)
                if tail:
                    attn_hi(p)
                if own:
                    et_copy(t, 3)
                    et_copy(t, 4)
                    av_copy(t, 0)
                if front:
                    q_hi(n, 1 - par)
                if own:
                    et_copy(t, 5)
                    exps(t, 3)
                if front:
                    v_copy(n, 1 - par)
                if own:
                    et_copy(t, 6)
                if ahead:
                    ctx_hi(n + 1)
                if own:
                    et_copy(t, 7)
                if front:
                    exps(n, 0)

            steps(step, act)

        @block.vector
        def _(dve):
            def stats(m, r, par):
                dve.wait_ge(sem.x_loaded[par], 16 * (r + 1))
                dve.bn_stats(b.bn[:, :], b.x[par][:, :]).then_inc(sem.bn_done, 1)

            def mean_variance():
                dve.bn_aggr(b.mv[:, :], b.bn[:, :]).then_inc(sem.stats_done, 1)

            def normalise(m, par):
                dve.wait_ge(sem.rstd_done, m + 1)
                wait(dve, sem.xT_done, m)
                dve.tensor_scalar(b.xn[:, :], b.x[par][:, :], b.mv[:, 0:1], b.rstd[:, 0:1], ALU.subtract,
                                  ALU.mult).then_inc(sem.xn_done, 1)

            def low_part(source, high, low, high_done, n, low_done):
                dve.wait_ge(high_done, n + 1)
                dve.tensor_tensor(low, source, high.bitcast(F32), ALU.subtract).then_inc(low_done, 1)

            def tiled(bank, k=KD):
                return bank[:, 0:k * P].rearrange("p (k n) -> p k n", k=k)

            def ctx_lo(n):
                low_part(tiled(MB, KC), b.cT[0][:, :, :], b.cT[1][:, :, :], sem.chi_done, n, sem.clo_done)

            def x_lo(n):
                low_part(tiled(MB), b.xT[0][:, :, :], b.xT[1][:, :, :], sem.xhi_done, n, sem.xlo_done)

            def k_lo(n):
                low_part(tiled(MB), b.kT[:, 0, :, :], b.kT[:, 1, :, :], sem.khi_done, n, sem.klo_done)

            def q_lo(n, par):
                low_part(tiled(MA), b.qT[par][0][:, :, :], b.qT[par][1][:, :, :], sem.qhi_done, n, sem.qlo_done)

            def attn_lo(p):
                low_part(tiled(MB), b.aT[0][:, :, :], b.aT[1][:, :, :], sem.ahi_done, p, sem.alo_done)

            def rope_products(bank, n, which, projected, added, done):
                dve.wait_ge(projected, n + 1)
                wait(dve, added, n)
                table = (c.cos, c.sin)
                cos, sin = (x[:, bass.ds(n, 1), :, :].rearrange("p a e i -> p a (e i)").broadcast_to([P, HEADS, HD])
                            for x in table)
                dve.tensor_tensor(b.rope[which][0][:, :].rearrange("p (h d) -> p h d", d=HD),
                                  bank[:, :].rearrange("p (h d) -> p h d", d=HD), cos, ALU.mult)
                swapped = bank[:, :].rearrange("p (h e i) -> p h e i", e=2, i=HD // 2)[:, :, ::-1, :]
                dve.tensor_tensor(b.rope[which][1][:, :].rearrange("p (h e i) -> p h e i", e=2, i=HD // 2),
                                  swapped, sin.rearrange("p h (e i) -> p h e i", e=2), ALU.mult).then_inc(done, 1)

            def rope_k(n):
                rope_products(MA, n, 0, sem.k_done, sem.kr_done, sem.kmul_done)

            def rope_q(n):
                rope_products(MA, n, 1, sem.q_done, sem.qr_done, sem.qmul_done)

            def softmax_shift(t, g):
                G = 4 * t + g
                bank = S[g % 2][:, :].rearrange("p (h k) -> p h k", k=P)
                dve.wait_ge(sem.s_done, G + 1)
                dve.reduce_max(b.mx[g % 2][:, :], bank, AX.X).then_inc(sem.mx_done, 1)
                dve.wait_ge(sem.mx_done, G + 1)
                wait(dve, sem.et_done, 2 * G - 2)
                dve.tensor_tensor(b.e[g % 2][:, :].rearrange("p (h k) -> p h k", k=P), bank,
                                  b.mx[g % 2][:, :].unsqueeze(2).broadcast_to([P, HPT, P]),
                                  ALU.subtract).then_inc(sem.sub_done, 1)

            def divide(p, half):
                H = 2 * p + half
                bank = (MB, MA)[half][:, :].rearrange("p (h d) -> p h d", d=2 * HD)
                dve.wait_ge(sem.outT_done, H + 1)
                dve.reciprocal(b.rsum[half][:, :], bank[:, :, HD]).then_inc(sem.rsum_done, 1)
                dve.wait_ge(sem.rsum_done, H + 1)
                wait(dve, sem.attnT_done, p)
                dve.tensor_tensor(b.attn[:, half, :].rearrange("p (h d) -> p h d", d=HD), bank[:, :, 0:HD],
                                  b.rsum[half][:, :].unsqueeze(2).broadcast_to([P, HEADS // 2, HD]),
                                  ALU.mult).then_inc(sem.norm_done, 1)

            def residual(p, r, par):
                dve.wait_ge(sem.o_done, p + 1)
                dve.wait_ge(sem.xb_done, p + 1)
                wait(dve, sem.x1_stored[par], 16 * r)
                dve.tensor_tensor(b.x1[par][:, :], MA[:, :], b.xb[par][:, :], ALU.add).then_inc(sem.x1_done, 1)

            stats(0, 0, 0)
            dve.wait_ge(sem.bn_done, 1)
            mean_variance()
            normalise(0, 0)
            ctx_lo(0)
            unpack_nibbles(dve, sem, c.dn_packed, c.dn_val, c.dn_sgn, 0, 0)
            rope_k(0)
            x_lo(0)
            stats(1, 0, 1)
            dve.wait_ge(sem.bn_done, 2)
            mean_variance()
            k_lo(0)
            unpack_nibbles(dve, sem, c.dn_packed, c.dn_val, c.dn_sgn, 1, 1)
            rope_q(0)
            for j in (2, 3):
                unpack_nibbles(dve, sem, c.dn_packed, c.dn_val, c.dn_sgn, j, j)
            normalise(1, 1)
            ctx_lo(1)
            q_lo(0, 0)
            softmax_shift(0, 0)

            def step(t, r, par):
                tail, own, front, ahead = stages(t)
                n, p = t + 1, t - 1
                if own:
                    softmax_shift(t, 1)
                if tail:
                    divide(p, 0)
                if front:
                    rope_k(n)
                    x_lo(n)
                if tail:
                    divide(p, 1)
                if own:
                    softmax_shift(t, 2)
                if front:
                    k_lo(n)
                    rope_q(n)
                if ahead:
                    stats(t + 2, r + 1, par)
                    dve.wait_ge(sem.bn_done, t + 3)
                if tail:
                    attn_lo(p)
                if ahead:
                    mean_variance()
                if own:
                    softmax_shift(t, 3)
                if front:
                    q_lo(n, 1 - par)
                    softmax_shift(n, 0)
                if ahead:
                    ctx_lo(n + 1)
                    normalise(t + 2, par)
                if tail:
                    residual(p, r + par - 1, 1 - par)

            steps(step, dve)

        @block.tensor
        def _(pe):
            def product(out, pairs, done):
                for i, (w, m) in enumerate(pairs):
                    last = nc.tensor.matmul(out, w, m, start=(i == 0), stop=(i == len(pairs) - 1))
                last.then_inc(done, 1)

            def three(w, m, k_tiles):
                return [(w(i, k), m(j, k)) for i, j in ((0, 1), (1, 0), (0, 0)) for k in range(k_tiles)]

            def ctx_transpose(n, r, par):
                pe.wait_ge(sem.ctx_loaded[par], 16 * (r + 1))
                wait(pe, sem.v_copied, n)
                for k in range(KC):
                    last = nc.tensor.transpose(MB[:, k * P:(k + 1) * P], b.ctx[par][:, k * P:(k + 1) * P],
                                               c.ident[:, :])
                last.then_inc(sem.ctxT_done, 1)

            def transpose4(bank, src, done):
                for k in range(KD):
                    last = nc.tensor.transpose(bank[:, k * P:(k + 1) * P], src[:, k * P:(k + 1) * P], c.ident[:, :])
                last.then_inc(done, 1)

            def out_transpose(p, half, own, front):
                H = 2 * p + half
                pe.wait_ge(sem.av_copied, H + 1)
                if half == 0:
                    if front:
                        pe.wait_ge(sem.clo_done, p + 3)
                    elif own:
                        pe.wait_ge(sem.v_copied, p + 2)
                elif front:
                    pe.wait_ge(sem.kmul_done, p + 3)
                else:
                    pe.wait_ge(sem.x1_done, p)
                transpose4((MB, MA)[half], b.avT[half], sem.outT_done)

            def k_project(n):
                pe.wait_ge(sem.clo_done, n + 1)
                wait(pe, sem.x1_done, n - 2)
                product(MA[:, :], three(lambda i, k: b.cT[i][:, k, :], lambda i, k: c.wkv[i][:, k, 0:DIM], KC),
                        sem.k_done)

            def v_project(n, tail):
                if tail:
                    pe.wait_ge(sem.alo_done, n - 1)
                else:
                    pe.wait_ge(sem.klo_done, n + 1)
                product(MB[:, :], three(lambda i, k: b.cT[i][:, k, :], lambda i, k: c.wkv[i][:, k, DIM:2 * DIM], KC),
                        sem.v_done)

            def q_project(n, tail):
                pe.wait_ge(sem.xlo_done, n + 1)
                if tail:
                    pe.wait_ge(sem.norm_done, 2 * n - 2)
                else:
                    pe.wait_ge(sem.kmul_done, n + 1)
                product(MA[:, :], three(lambda i, k: b.xT[i][:, k, :], lambda i, k: c.wq[i][:, k, :], KD), sem.q_done)

            def x_transpose(n, tail):
                pe.wait_ge(sem.xn_done, n + 1)
                if tail:
                    pe.wait_ge(sem.norm_done, 2 * n - 3)
                else:
                    pe.wait_ge(sem.clo_done, n + 1)
                transpose4(MB, b.xn, sem.xT_done)

            def k_transpose(n):
                pe.wait_ge(sem.kr_done, n + 1)
                pe.wait_ge(sem.xlo_done, n + 1)
                transpose4(MB, b.kr, sem.kT_done)

            def q_transpose(n):
                pe.wait_ge(sem.qr_done, n + 1)
                transpose4(MA, b.qr, sem.qT_done)

            def scores(t, g, r, par):
                G = 4 * t + g
                wait(pe, sem.sub_done, G - 1)
                if g == 0:
                    pe.wait_ge(sem.kblk_ready[par], 16 * HPT * (r + 1))
                    pe.wait_ge(sem.qlo_done, t + 1)
                for half in range(2):
                    pairs = [(b.qT[par][i][:, g, :], b.kblk[par][:, 4 * half:4 * half + 4, j, g, :])
                             for i, j in ((0, 1), (1, 0), (0, 0))]
                    for i, (w, m) in enumerate(pairs):
                        last = nc.tensor.matmul(S[g % 2][:, 512 * half:512 * half + 512], w, m, start=(i == 0), stop=(i == 2))
                last.then_inc(sem.s_done, 1)

            def e_transpose(t, u):
                U = UNITS * t + u
                if u % 2 == 0:
                    pe.wait_ge(sem.exp_done, 4 * t + u // 2 + 1)
                wait(pe, sem.et_copied, U)
                transpose4(ET, b.e[u // 2 % 2][:, 512 * (u % 2):512 * (u % 2) + 512], sem.et_done)

            def values(t, u, par):
                U = UNITS * t + u
                pe.wait_ge(sem.et_copied, U + 1)
                if u == 0:
                    pe.wait_ge(sem.v_copied, t + 1)
                if u % 4 == 0:
                    wait(pe, sem.av_copied, 2 * t + u // 4)
                for i in range(4):
                    last = nc.tensor.matmul(AV[32 * i:32 * i + 32, (u % 4) * P:(u % 4 + 1) * P],
                                            b.v[par][:, 4 * u + i, :], b.et[u % 2][:, i * P:(i + 1) * P],
                                            start=True, stop=True)
                last.then_inc(sem.av_done, 1)

            def attn_transpose(p, front):
                pe.wait_ge(sem.norm_done, 2 * p + 2)
                if front:
                    pe.wait_ge(sem.klo_done, p + 3)
                for k in range(KD):
                    last = nc.tensor.transpose(MB[:, k * P:(k + 1) * P],
                                               b.attn[:, k // 2, (k % 2) * P:(k % 2 + 1) * P], c.ident[:, :])
                last.then_inc(sem.attnT_done, 1)

            def out_project(p, front):
                pe.wait_ge(sem.alo_done, p + 1)
                if front:
                    pe.wait_ge(sem.qlo_done, p + 3)
                product(MA[:, :], three(lambda i, k: b.aT[i][:, k, :], lambda i, k: c.wo[i][:, k, :], KD), sem.o_done)

            ctx_transpose(0, 0, 0)
            k_project(0)
            x_transpose(0, False)
            k_transpose(0)
            q_project(0, False)
            v_project(0, False)
            ctx_transpose(1, 0, 1)
            q_transpose(0)
            scores(0, 0, 0, 0)

            def step(t, r, par):
                tail, own, front, ahead = stages(t)
                n, p = t + 1, t - 1
                if own:
                    scores(t, 1, r, par)
                if tail:
                    values(p, 7, 1 - par)
                if front:
                    k_project(n)
                if tail:
                    out_transpose(p, 0, own, front)
                if own:
                    e_transpose(t, 0)
                    scores(t, 2, r, par)
                if front:
                    x_transpose(n, tail)
                if own:
                    e_transpose(t, 1)
                    values(t, 0, par)
                if tail:
                    out_transpose(p, 1, own, front)
                if own:
                    e_transpose(t, 2)
                if front:
                    k_transpose(n)
                    q_project(n, tail)
                if own:
                    e_transpose(t, 3)
                    values(t, 1, par)
                if tail:
                    attn_transpose(p, front)
                if own:
                    values(t, 2, par)
                    scores(t, 3, r, par)
                    e_transpose(t, 4)
                if front:
                    q_transpose(n)
                if own:
                    values(t, 3, par)
                    e_transpose(t, 5)
                if front:
                    v_project(n, tail)
                if own:
                    values(t, 4, par)
                    values(t, 5, par)
                    e_transpose(t, 6)
                if front:
                    scores(n, 0, r + par, 1 - par)
                if ahead:
                    ctx_transpose(n + 1, r + 1, par)
                if tail:
                    out_project(p, front)
                if own:
                    e_transpose(t, 7)
                    values(t, 6, par)

            steps(step, pe)


def by_nibble(x):
    return x.rearrange("p (w j h) -> p w h j", j=4, h=2)


class FirstNorm:

    def __init__(self, nc, sem, c, b, ps_z, x1_dram):
        self.nc, self.sem, self.c, self.b, self.ps_z, self.x1_dram = nc, sem, c, b, ps_z, x1_dram

    def load(self, sp, m, par):
        sp.dma_start(self.b.x[par][:, :, :], self.x1_dram[bass.ds(CHUNK * m, CHUNK), :, :].rearrange(
            "t p n -> p t n")).then_inc(self.sem.f_loaded[par], 16)

    def stats(self, dve, m, r, par, j):
        if j == 0:
            dve.wait_ge(self.sem.f_loaded[par], 16 * (r + 1))
        last = dve.bn_stats(self.b.bn[:, j, :], self.b.x[par][:, j, :])
        if j == CHUNK - 1:
            last.then_inc(self.sem.f_bn_done, 1)

    def mean_variance(self, dve):
        for j in range(CHUNK):
            last = dve.bn_aggr(self.b.mv[:, j, :], self.b.bn[:, j, :])
        last.then_inc(self.sem.f_stats_done, 1)

    def rstd(self, pool, m):
        sem, b, c = self.sem, self.b, self.c
        pool.wait_ge(sem.f_stats_done, m + 1)
        pool.tensor_tensor(b.rstd[:, :], b.mv[:, :, 1], c.ln_eps[:, 0:1].broadcast_to([P, CHUNK]),
                           ALU.add).then_inc(sem.f_vareps_done, 1)
        pool.wait_ge(sem.f_vareps_done, m + 1)
        pool.tensor_tensor(b.rstd[:, :], b.rstd[:, :], c.minus_half[:, 0:1].broadcast_to([P, CHUNK]),
                           ALU.pow).then_inc(sem.f_rstd_done, 1)

    def normalise(self, dve, m, par, j):
        sem, b = self.sem, self.b
        if j == 0:
            dve.wait_ge(sem.f_rstd_done, m + 1)
        wait(dve, sem.zT_done, CHUNK * m + j - 1)
        dve.tensor_scalar(by_nibble(b.z[j % 2][:, :]), b.x[par][:, j, :].rearrange("p (w h j) -> p w h j", h=2, j=4),
                          b.mv[:, j, 0:1], b.rstd[:, j:j + 1], ALU.subtract, ALU.mult).then_inc(sem.z_done, 1)

    def transpose(self, pe, m, j):
        sem, b = self.sem, self.b
        pe.wait_ge(sem.z_done, CHUNK * m + j + 1)
        wait(pe, sem.zlo_done, CHUNK * m + j)
        for k in range(KD):
            last = self.nc.tensor.transpose(self.ps_z[:, k * P:(k + 1) * P], b.z[j % 2][:, k * P:(k + 1) * P],
                                            self.c.ident[:, :])
        last.then_inc(sem.zT_done, 1)

    def high(self, act, m, par, j):
        act.wait_ge(self.sem.zT_done, CHUNK * m + j + 1)
        act.activation(self.b.zT[par][0][:, :, j * P:(j + 1) * P],
                       self.ps_z[:, :].rearrange("p (k n) -> p k n", k=KD), ACT.Copy).then_inc(self.sem.zhi_done, 1)

    def low(self, dve, m, par, j):
        dve.wait_ge(self.sem.zhi_done, CHUNK * m + j + 1)
        dve.tensor_tensor(self.b.zT[par][1][:, :, j * P:(j + 1) * P],
                          self.ps_z[:, :].rearrange("p (k n) -> p k n", k=KD),
                          self.b.zT[par][0][:, :, j * P:(j + 1) * P].bitcast(F32),
                          ALU.subtract).then_inc(self.sem.zlo_done, 1)


def ffn_weights(nc, sem, c, w, tmp, ps, norm, A_gus, A_dns):
    FT = len(ps.fT)
    FW = len(tmp.fw)
    gu_tiles = 2 * INTER // P
    cut = gu_tiles // 8 * 4 + 4
    parts = ((0, cut), (cut, gu_tiles))
    gu = [[(g, o, min(4, last - o)) for g in range(KD) for o in range(first, last, 4)] for first, last in parts]

    def unpack(part, j):
        return [("unpack", part, j)]

    def gate_up(part, first, last):
        return [("gu", part, u) for u in range(first, last)]

    def down(first, last):
        return [("dn", 0, g) for g in range(first, last)]

    third = len(gu[0]) // 3
    order = (unpack(0, 0) + unpack(0, 1) + [("stats", 0, 0)] + unpack(0, 2) + [("variance", 0, 0)] + unpack(0, 3)
             + down(0, 2) + [("norm", 0, 0), ("norm", 0, 1)] + down(2, 3) + [("zT", 0, 0)] + down(3, 4)
             + unpack(1, 0) + gate_up(0, 0, third) + [("zT", 0, 1), ("norm", 0, 2)] + down(4, 6)
             + unpack(1, 1) + gate_up(0, third, 2 * third) + [("zT", 0, 2), ("norm", 0, 3)] + down(6, 8)
             + unpack(1, 2) + gate_up(0, 2 * third, len(gu[0])) + [("zT", 0, 3)] + down(8, 9)
             + unpack(1, 3) + down(9, KI) + gate_up(1, 0, len(gu[1])))
    units = [kind for kind, _, _ in order if kind in ("gu", "dn")]

    with nc.Block() as block:

        @block.sync
        def _(sp):
            norm.load(sp, 0, 0)
            sp.dma_start(tmp.gu_scale[:, :], A_gus).then_inc(sem.gu_scale_loaded, 16)

        @block.scalar
        def _(act):
            act.dma_start(tmp.dn_scale[:, :, :], A_dns.rearrange("(a g) o -> a g o", a=1).broadcast_to(
                [P, KI, DIM])).then_inc(sem.dn_scale_loaded, 16)
            act.wait_ge(sem.gu_scale_loaded, 16)
            act.activation(by_nibble(tmp.gu_scale_sorted[:, :]),
                           tmp.gu_scale[:, :].rearrange("p (w h j) -> p w h j", h=2, j=4),
                           ACT.Copy).then_inc(sem.scale_sorted, 1)
            i = 0
            for kind, part, n in order:
                if kind == "zT":
                    norm.high(act, 0, 0, n)
                if kind == "gu":
                    g, o, tiles = gu[part][n]
                    act.wait_ge(sem.fT_done, i + 1)
                    act.activation(by_nibble(w.gu[:, g, o * P:(o + tiles) * P]),
                                   ps.fT[i % FT][:, :].bitcast(F16)[:, 0:tiles * P].rearrange(
                                       "p (w h j) -> p w h j", h=2, j=4),
                                   ACT.Copy, scale=16384.0).then_inc(sem.fv_done, 1)
                if kind == "dn":
                    act.wait_ge(sem.fw_done, n + 1)
                    act.activation(w.dn[0][:, n, :], tmp.fw[n % FW][:, :], ACT.Copy).then_inc(sem.fhi_done, 1)
                if kind in ("gu", "dn"):
                    i += 1
            act.wait_ge(sem.sT_done, 1)
            act.activation(c.gu_scale[:, :, :], ps.scales[:, :].bitcast(F16)[:, 0:gu_tiles * KD].rearrange(
                "p (t g) -> p t g", g=KD), ACT.Copy).then_inc(sem.sT_copied, 1)
            act.wait_ge(sem.sT_copied, 1)

        @block.gpsimd
        def _(pool):
            norm.rstd(pool, 0)
            for g in range(KI):
                pool.wait_ge(sem.fhi_done, g + 1)
                pool.tensor_tensor(w.dn[1][:, g, :], tmp.fw[g % FW][:, :], w.dn[0][:, g, :].bitcast(F32),
                                   ALU.subtract).then_inc(sem.flo_done, 1)
            pool.wait_ge(sem.flo_done, KI)

        @block.vector
        def _(dve):
            i = 0
            for kind, part, n in order:
                if kind == "unpack":
                    first, last = parts[part]
                    unpack_nibbles(dve, sem, c.gu_packed[:, first:last, :], tmp.gu_val[:, first:last, :, :],
                                   tmp.gu_sgn[:, first:last, :], n, 4 * (part + 1) + n)
                if kind == "stats":
                    for j in range(CHUNK):
                        norm.stats(dve, 0, 0, 0, j)
                    dve.wait_ge(sem.f_bn_done, 1)
                if kind == "variance":
                    norm.mean_variance(dve)
                if kind == "norm":
                    norm.normalise(dve, 0, 0, n)
                if kind == "zT":
                    norm.low(dve, 0, 0, n)
                if kind == "dn":
                    if n == 0:
                        dve.wait_ge(sem.dn_scale_loaded, 16)
                    dve.wait_ge(sem.fT_done, i + 1)
                    if n >= FW:
                        dve.wait_ge(sem.flo_done, n - FW + 1)
                    dve.scalar_tensor_tensor(out=tmp.fw[n % FW][:, :],
                                             in0=ps.fT[i % FT][:, :].bitcast(F16)[:, 0:DIM],
                                             scalar=16384.0, in1=tmp.dn_scale[:, n, :], op0=ALU.mult,
                                             op1=ALU.mult).then_inc(sem.fw_done, 1)
                if kind in ("gu", "dn"):
                    i += 1

        @block.tensor
        def _(pe):
            i = 0
            for kind, part, n in order:
                if kind == "zT":
                    norm.transpose(pe, 0, n)
                if kind == "dn" and n == KI - 1:
                    pe.wait_ge(sem.scale_sorted, 1)
                    for k in range(gu_tiles):
                        last = nc.tensor.transpose(ps.scales[:, :].bitcast(F16)[:, k * KD:(k + 1) * KD],
                                                   tmp.gu_scale_sorted[:, k * P:(k + 1) * P], c.ident16[0:KD, 0:KD])
                    last.then_inc(sem.sT_done, 1)
                if kind in ("gu", "dn"):
                    value, (g, o, tiles) = (tmp.gu_val, gu[part][n]) if kind == "gu" else (c.dn_val, (n, 0, KD))
                    if kind == "gu":
                        pe.wait_ge(sem.or_done, 4 * (part + 2))
                    if i >= FT:
                        read = sem.fv_done if units[i - FT] == "gu" else sem.fw_done
                        pe.wait_ge(read, units[0:i - FT + 1].count(units[i - FT]))
                    for k in range(tiles):
                        rows = value[:, o + k, 16 * g:16 * g + 16, :].rearrange("p w j -> p (w j)").bitcast(F16)
                        last = nc.tensor.transpose(ps.fT[i % FT][:, :].bitcast(F16)[:, k * P:(k + 1) * P], rows,
                                                   c.ident16[:, :])
                    last.then_inc(sem.fT_done, 1)
                    i += 1


def ffn(nc, sem, c, w, b, ps, norm, out, tiles):
    chunks = tiles // CHUNK
    PRODUCTS = 2 * KD * KI
    BANKS = len(ps.sums)
    RING = 3

    def steps(step, engine):
        step(0, 0, 0)
        step(1, 0, 1)
        with engine.Fori(1, chunks // 2 - 1) as r:
            step(2 * r, r, 0)
            step(2 * r + 1, r, 1)
        step(chunks - 2, chunks // 2 - 1, 0)
        step(chunks - 1, chunks // 2 - 1, 1)
        step(chunks, chunks // 2, 0)

    def stages(m):
        if isinstance(m, int):
            return m >= 1, m < chunks, m + 1 < chunks
        return True, True, True

    def before(m, i):
        if i > 0:
            return (m, i - 1) if stages(m)[1] else None
        return (m - 1, KI - 1) if stages(m)[0] else None

    def last_in_ring(i, size, count):
        if i >= size:
            return i - size
        return max(x for x in range(count) if x % size == i) - count

    def ring_count(m, i):
        return KI * m + last_in_ring(i, RING, KI) + 1

    def product_parts(i, kind, g):
        q = 2 * KD * i + KD * kind + g
        bank = ps.z if q == PRODUCTS - 1 else ps.sums[q % BANKS]
        return q, bank, b.part[kind][g // 2][i % RING], c.gu_scale[:, kind * KI + i, g:g + 1]

    with nc.Block() as block:

        @block.sync
        def _(sp):
            def step(m, r, par):
                prev, cur, more = stages(m)
                if prev:
                    for j in range(CHUNK):
                        sp.wait_ge(sem.f_out_done, CHUNK * (m - 1) + j + 1)
                        sp.dma_start(out[bass.ds(CHUNK * (m - 1) + j, 1), :, :].rearrange("a p n -> p (a n)"),
                                     b.x[1 - par][:, j, :]).then_inc(sem.f_stored[1 - par], 16)
                if more:
                    wait(sp, sem.f_stored[1 - par], 16 * CHUNK * (r + par))
                    norm.load(sp, m + 1, 1 - par)

            steps(step, sp)
            for par in range(2):
                sp.wait_ge(sem.f_stored[par], 16 * CHUNK * (chunks // 2))

        @block.gpsimd
        def _(pool):
            def add_halves(m, i, kind):
                pool.wait_ge(sem.dve_scaled, PRODUCTS // 2 * m + KD * i + KD // 2 * (kind + 1))
                x = b.part[kind][0][i % RING]
                pool.tensor_tensor(x[:, :], x[:, :], b.part[kind][1][i % RING][:, :],
                                   ALU.add).then_inc(sem.up_added if kind else sem.gate_added, 1)

            def h_low(m, i):
                pool.wait_ge(sem.hhi_done, KI * m + i + 1)
                pool.tensor_tensor(b.h[1][i % RING][:, :], b.part[0][0][i % RING][:, :],
                                   b.h[0][i % RING][:, :].bitcast(F32), ALU.subtract).then_inc(sem.hlo_done, 1)

            def rrms(m, j):
                M = CHUNK * m + j
                rr = b.rrms[:, j:j + 1]
                pool.wait_ge(sem.square_done, M + 1)
                wait(pool, sem.f_out_done, M + 1 - CHUNK)
                pool.tensor_tensor(rr, b.ssq[:, j:j + 1], c.rms_eps[:, :], ALU.add).then_inc(sem.ms_done, 1)
                pool.wait_ge(sem.ms_done, M + 1)
                pool.tensor_tensor(rr, rr, c.minus_half[:, :], ALU.pow).then_inc(sem.rrms_done, 1)

            def step(m, r, par):
                prev, cur, more = stages(m)
                for i in range(KI if cur else 3):
                    if before(m, i):
                        add_halves(*before(m, i), 1)
                    if prev and i in (1, 2):
                        rrms(m - 1, 0 if i == 1 else 3)
                    if before(m, i):
                        h_low(*before(m, i))
                    if prev and i == 1:
                        rrms(m - 1, 1)
                    if cur:
                        add_halves(m, i, 0)
                    if prev and i == 1:
                        rrms(m - 1, 2)
                    if more and i == 5:
                        norm.rstd(pool, m + 1)

            steps(step, pool)

        @block.scalar
        def _(act):
            def scaled(m, i, kind, g):
                q, bank, part, scale = product_parts(i, kind, g)
                if kind == 0:
                    wait(act, sem.hlo_done if g == 0 else sem.gate_added, ring_count(m, i))
                else:
                    wait(act, sem.mul_done if g == 0 else sem.up_added, ring_count(m, i))
                act.wait_ge(sem.product_done, PRODUCTS * m + q + 1)
                act.activation(part[:, :], bank[:, :], ACT.Copy, scale=scale).then_inc(sem.act_scaled, 1)

            def silu(m, i):
                act.wait_ge(sem.gate_added, KI * m + i + 1)
                x = b.part[0][0][i % RING]
                act.activation(x[:, :], x[:, :], ACT.Silu).then_inc(sem.silu_done, 1)

            def h_high(m, i):
                act.wait_ge(sem.mul_done, KI * m + i + 1)
                back = last_in_ring(i, RING, KI)
                if back == -1:
                    wait(act, sem.y_done, CHUNK * m)
                elif back < 0:
                    wait(act, sem.down_done, (KI - 1) * (m - 1) + KI + back + 1)
                else:
                    act.wait_ge(sem.down_done, (KI - 1) * m + back + 1)
                act.activation(b.h[0][i % RING][:, :], b.part[0][0][i % RING][:, :], ACT.Copy).then_inc(
                    sem.hhi_done, 1)

            def square(m, j):
                act.wait_ge(sem.y_done, CHUNK * m + j + 1)
                wait(act, sem.rrms_done, CHUNK * (m - 1) + j + 1)
                wait(act, sem.square_done, CHUNK * m + j - 1)
                act.activation(b.junk[j % 2][:, :], ps.y[j][:, :], ACT.Square, scale=DIM ** -0.5,
                               accum_out=b.ssq[:, j:j + 1]).then_inc(sem.square_done, 1)

            def step(m, r, par):
                prev, cur, more = stages(m)
                for i in range(KI if cur else 3):
                    if cur:
                        scaled(m, i, 0, 0)
                    if prev and i in (1, 2):
                        square(m - 1, 0 if i == 1 else 3)
                    if cur:
                        scaled(m, i, 0, 2)
                    if before(m, i):
                        h_high(*before(m, i))
                    if prev and i == 1:
                        square(m - 1, 1)
                    if more and i >= KI - CHUNK:
                        norm.high(act, m + 1, 1 - par, i - (KI - CHUNK))
                    if cur:
                        scaled(m, i, 1, 0)
                    if prev and i == 1:
                        square(m - 1, 2)
                    if cur:
                        scaled(m, i, 1, 2)
                        silu(m, i)

            steps(step, act)

        @block.vector
        def _(dve):
            def scaled_sum(m, i, kind, g):
                q, bank, part, scale = product_parts(i, kind, g)
                dve.wait_ge(sem.act_scaled, PRODUCTS // 2 * m + q // 2 + 1)
                dve.wait_ge(sem.product_done, PRODUCTS * m + q + 1)
                dve.scalar_tensor_tensor(out=part[:, :], in0=bank[:, :], scalar=scale, in1=part[:, :],
                                         op0=ALU.mult, op1=ALU.add).then_inc(sem.dve_scaled, 1)

            def gate_times_up(m, i):
                dve.wait_ge(sem.up_added, KI * m + i + 1)
                dve.wait_ge(sem.silu_done, KI * m + i + 1)
                x = b.part[0][0][i % RING]
                dve.tensor_tensor(x[:, :], x[:, :], b.part[1][0][i % RING][:, :], ALU.mult).then_inc(sem.mul_done, 1)

            def residual(m, par, j):
                dve.wait_ge(sem.rrms_done, CHUNK * m + j + 1)
                dve.scalar_tensor_tensor(out=b.x[par][:, j, :], in0=ps.y[j][:, :], scalar=b.rrms[:, j:j + 1],
                                         in1=b.x[par][:, j, :], op0=ALU.mult, op1=ALU.add).then_inc(sem.f_out_done, 1)

            def step(m, r, par):
                prev, cur, more = stages(m)
                for i in range(KI if cur else 3):
                    if more and i == 5:
                        dve.wait_ge(sem.f_bn_done, m + 2)
                    if cur:
                        scaled_sum(m, i, 0, 1)
                    if more and i == 5:
                        norm.mean_variance(dve)
                    if before(m, i):
                        gate_times_up(*before(m, i))
                    if prev and i == 2:
                        residual(m - 1, 1 - par, 3)
                    if cur:
                        scaled_sum(m, i, 0, 3)
                    if prev and i == 1:
                        residual(m - 1, 1 - par, 0)
                    if more and i >= KI - CHUNK:
                        norm.low(dve, m + 1, 1 - par, i - (KI - CHUNK))
                    if cur:
                        scaled_sum(m, i, 1, 1)
                    if prev and i == 1:
                        residual(m - 1, 1 - par, 1)
                    if cur:
                        scaled_sum(m, i, 1, 3)
                    if prev and i == 1:
                        residual(m - 1, 1 - par, 2)
                    if more and i in (3, 4):
                        for j in range(2):
                            norm.stats(dve, m + 1, r + par, 1 - par, 2 * (i - 3) + j)
                    if more and KI - CHUNK - 1 <= i < KI - 1:
                        norm.normalise(dve, m + 1, 1 - par, i - (KI - CHUNK - 1))

            steps(step, dve)

        @block.tensor
        def _(pe):
            def product(m, i, kind, g, par):
                q, bank, _, _ = product_parts(i, kind, g)
                if q == PRODUCTS - 1:
                    if stages(m)[2]:
                        pe.wait_ge(sem.zlo_done, CHUNK * (m + 2))
                else:
                    back = last_in_ring(q, BANKS, PRODUCTS - 1)
                    if back < 0:
                        back -= 1
                    read = sem.dve_scaled if back % 2 else sem.act_scaled
                    wait(pe, read, PRODUCTS // 2 * m + back // 2 + 1)
                column = kind * INTER + i * P
                nc.tensor.matmul(bank[:, :], w.gu[:, g, column:column + P], b.zT[par][1][:, g, :], start=True,
                                 stop=False)
                nc.tensor.matmul(bank[:, :], w.gu[:, g, column:column + P], b.zT[par][0][:, g, :], start=False,
                                 stop=True).then_inc(sem.product_done, 1)

            def down(m, k, j):
                if j == 0:
                    pe.wait_ge(sem.hlo_done, KI * m + k + 1)
                if k == 0:
                    wait(pe, sem.f_out_done, CHUNK * (m - 1) + j + 1)
                for a, x in ((0, 1), (1, 0), (0, 0)):
                    last = nc.tensor.matmul(ps.y[j][:, :], b.h[a][k % RING][:, j * P:(j + 1) * P], w.dn[x][:, k, :],
                                            start=(k == 0 and (a, x) == (0, 1)),
                                            stop=(k == KI - 1 and (a, x) == (0, 0)))
                if k == KI - 1:
                    last.then_inc(sem.y_done, 1)
                elif j == CHUNK - 1:
                    last.then_inc(sem.down_done, 1)

            def step(m, r, par):
                prev, cur, more = stages(m)
                for i in range(KI if cur else 2):
                    if cur and i == 0:
                        pe.wait_ge(sem.zlo_done, CHUNK * m + CHUNK)
                    for n in range(2 * KD):
                        if more and i == KI - CHUNK and n == 2:
                            wait(pe, sem.dve_scaled, PRODUCTS // 2 * m)
                        if more and i >= KI - CHUNK and n == 2:
                            norm.transpose(pe, m + 1, i - (KI - CHUNK))
                        if cur:
                            product(m, i, n // KD, n % KD, par)
                        if n % 2 == 1:
                            if i >= 2:
                                down(m, i - 2, n // 2)
                            elif prev:
                                down(m - 1, KI + i - 2, n // 2)

            steps(step, pe)


def program(nc, A_x, A_ctx, A_pos, A_wq, A_wkv, A_wo, A_bout, A_gu, A_gus, A_dn, A_dns, out):
    tiles = A_x.shape[0]
    x1_dram = nc.dram_tensor("x1_scratch", [tiles, P, DIM], F32, kind="Internal").ap()

    with ExitStack() as whole:
        def semaphore(name):
            return whole.enter_context(nc.semaphore(name))

        def semaphores(name):
            return [semaphore(f"{name}{i}") for i in range(2)]

        sem = Named()
        sem.pos_loaded = semaphore("pos_loaded")
        sem.wq_loaded = semaphore("wq_loaded")
        sem.wkv_loaded = semaphore("wkv_loaded")
        sem.wo_loaded = semaphore("wo_loaded")
        sem.bout_loaded = semaphore("bout_loaded")
        sem.const_set = semaphore("const_set")
        sem.w_hi = semaphore("w_hi")
        sem.w_lo = semaphore("w_lo")
        sem.angles = semaphore("angles")
        sem.tables = semaphore("tables")
        sem.setup_chain = semaphore("setup_chain")
        sem.kblk_zeroed = semaphore("kblk_zeroed")
        sem.v_zeroed = semaphore("v_zeroed")
        sem.v_ones = semaphore("v_ones")
        sem.klo_done = semaphore("klo_done")
        sem.khi_done = semaphore("khi_done")
        sem.s_done = semaphore("s_done")
        sem.xb_done = semaphore("xb_done")
        sem.ctxT_done = semaphore("ctxT_done")
        sem.x1_done = semaphore("x1_done")
        sem.stats_done = semaphore("stats_done")
        sem.vareps_done = semaphore("vareps_done")
        sem.rstd_done = semaphore("rstd_done")
        sem.kmul_done = semaphore("kmul_done")
        sem.qmul_done = semaphore("qmul_done")
        sem.kT_done = semaphore("kT_done")
        sem.qT_done = semaphore("qT_done")
        sem.kr_done = semaphore("kr_done")
        sem.qr_done = semaphore("qr_done")
        sem.v_done = semaphore("v_done")
        sem.q_done = semaphore("q_done")
        sem.k_done = semaphore("k_done")
        sem.xT_done = semaphore("xT_done")
        sem.chi_done = semaphore("chi_done")
        sem.xhi_done = semaphore("xhi_done")
        sem.qhi_done = semaphore("qhi_done")
        sem.qlo_done = semaphore("qlo_done")
        sem.v_copied = semaphore("v_copied")
        sem.sub_done = semaphore("sub_done")
        sem.exp_done = semaphore("exp_done")
        sem.et_done = semaphore("et_done")
        sem.et_copied = semaphore("et_copied")
        sem.av_done = semaphore("av_done")
        sem.av_copied = semaphore("av_copied")
        sem.outT_done = semaphore("outT_done")
        sem.attnT_done = semaphore("attnT_done")
        sem.ahi_done = semaphore("ahi_done")
        sem.alo_done = semaphore("alo_done")
        sem.o_done = semaphore("o_done")
        sem.bn_done = semaphore("bn_done")
        sem.xn_done = semaphore("xn_done")
        sem.clo_done = semaphore("clo_done")
        sem.xlo_done = semaphore("xlo_done")
        sem.mx_done = semaphore("mx_done")
        sem.rsum_done = semaphore("rsum_done")
        sem.norm_done = semaphore("norm_done")
        sem.gu_loaded = semaphore("gu_loaded")
        sem.dn_loaded = semaphore("dn_loaded")
        sem.dn_scale_loaded = semaphore("dn_scale_loaded")
        sem.fw_done = semaphore("fw_done")
        sem.fhi_done = semaphore("fhi_done")
        sem.flo_done = semaphore("flo_done")
        sem.nibbles_done = semaphore("nibbles_done")
        sem.or_done = semaphore("or_done")
        sem.fT_done = semaphore("fT_done")
        sem.f_out_done = semaphore("f_out_done")
        sem.f_stats_done = semaphore("f_stats_done")
        sem.f_vareps_done = semaphore("f_vareps_done")
        sem.f_rstd_done = semaphore("f_rstd_done")
        sem.f_bn_done = semaphore("f_bn_done")
        sem.hhi_done = semaphore("hhi_done")
        sem.hlo_done = semaphore("hlo_done")
        sem.square_done = semaphore("square_done")
        sem.ms_done = semaphore("ms_done")
        sem.rrms_done = semaphore("rrms_done")
        sem.silu_done = semaphore("silu_done")
        sem.mul_done = semaphore("mul_done")
        sem.zT_done = semaphore("zT_done")
        sem.zhi_done = semaphore("zhi_done")
        sem.zlo_done = semaphore("zlo_done")
        sem.z_done = semaphore("z_done")
        sem.y_done = semaphore("y_done")
        sem.down_done = semaphore("down_done")
        sem.product_done = semaphore("product_done")
        sem.act_scaled = semaphore("act_scaled")
        sem.dve_scaled = semaphore("dve_scaled")
        sem.gate_added = semaphore("gate_added")
        sem.up_added = semaphore("up_added")
        sem.scale_sorted = semaphore("scale_sorted")
        sem.sT_done = semaphore("sT_done")
        sem.sT_copied = semaphore("sT_copied")
        sem.fv_done = semaphore("fv_done")
        sem.x_loaded = semaphores("x_loaded")
        sem.ctx_loaded = semaphores("ctx_loaded")
        sem.kblk_ready = semaphores("kblk_ready")
        sem.x1_stored = semaphores("x1_stored")
        sem.f_loaded = semaphores("f_loaded")
        sem.f_stored = semaphores("f_stored")
        sem.gu_scale_loaded = semaphore("gu_scale_loaded")

        def sbuf(stack, name, shape, dt=F32):
            return stack.enter_context(nc.sbuf_tensor(name, shape, dt))

        def psum(stack, name, columns):
            return stack.enter_context(nc.psum_tensor(name, [P, columns], F32))

        c = Named()
        c.ident = sbuf(whole, "ident", [P, P])
        c.ident16 = sbuf(whole, "ident16", [P, P], F16)
        c.minus_half = sbuf(whole, "minus_half", [P, 1])
        c.ln_eps = sbuf(whole, "ln_eps", [P, 1])
        c.rms_eps = sbuf(whole, "rms_eps", [P, 1])

        c.gu_packed = sbuf(whole, "gu_packed", [P, 2 * INTER // P, DIM // 8], U32)
        c.dn_val = sbuf(whole, "dn_val", [P, KD, INTER // 8, 4], U32)
        c.gu_scale = sbuf(whole, "gu_scale_columns", [P, 2 * INTER // P, KD])

        with ExitStack() as phase:
            c.dn_packed = sbuf(phase, "dn_packed", [P, KD, INTER // 8], U32)
            c.dn_sgn = sbuf(phase, "dn_sgn", [P, KD, INTER // 8], U32)
            c.bout = sbuf(phase, "bout", [P, DIM])
            c.cos = sbuf(phase, "cos", [P, tiles, 2, HD // 2])
            c.sin = sbuf(phase, "sin", [P, tiles, 2, HD // 2])
            c.wq = [sbuf(phase, f"wq{i}", [P, KD, DIM], F32R) for i in range(2)]
            c.wkv = [sbuf(phase, f"wkv{i}", [P, KC, 2 * DIM], F32R) for i in range(2)]
            c.wo = [sbuf(phase, f"wo{i}", [P, KD, DIM], F32R) for i in range(2)]
            b = Named()
            b.kblk = [sbuf(phase, f"kblk{i}", [P, HPT, 2, KD, P], F32R) for i in range(2)]
            b.v = [sbuf(phase, f"v{i}", [P, HEADS, 2 * HD]) for i in range(2)]
            with ExitStack() as scratch:
                tmp = Named()
                tmp.pos = sbuf(scratch, "pos", [P, tiles, 2])
                tmp.ang = sbuf(scratch, "ang", [P, tiles, HD // 2])
                tmp.turns = sbuf(scratch, "turns", [P, tiles, HD // 2])
                tmp.ang_s = sbuf(scratch, "ang_s", [P, tiles, HD // 2])
                tmp.ang_c = sbuf(scratch, "ang_c", [P, tiles, HD // 2])
                tmp.wq = sbuf(scratch, "wq_raw", [P, KD, DIM])
                tmp.wkv = sbuf(scratch, "wkv_raw", [P, KC, 2 * DIM])
                tmp.wo = sbuf(scratch, "wo_raw", [P, KD, DIM])
                setup_constants(nc, sem, c, b, tmp, A_pos, A_wq, A_wkv, A_wo, A_bout, A_gu, A_dn, tiles)

            b.x = [sbuf(phase, f"x{i}", [P, DIM]) for i in range(2)]
            b.ctx = [sbuf(phase, f"ctx{i}", [P, CTX]) for i in range(2)]
            b.xb = [sbuf(phase, f"xb{i}", [P, DIM]) for i in range(2)]
            b.x1 = [sbuf(phase, f"x1_{i}", [P, DIM]) for i in range(2)]
            b.bn = sbuf(phase, "bn", [P, 6])
            b.mv = sbuf(phase, "mv", [P, 2])
            b.rstd = sbuf(phase, "rstd", [P, 1])
            b.xn = sbuf(phase, "xn", [P, DIM])
            b.xT = [sbuf(phase, f"xT{i}", [P, KD, P], F32R) for i in range(2)]
            b.cT = [sbuf(phase, f"cT{i}", [P, KC, P], F32R) for i in range(2)]
            b.rope = [[sbuf(phase, f"rope{w}{i}", [P, DIM]) for i in range(2)] for w in "kq"]
            b.kr = sbuf(phase, "kr", [P, DIM])
            b.qr = sbuf(phase, "qr", [P, DIM])
            b.kT = sbuf(phase, "kT", [P, 2, KD, P], F32R)
            b.qT = [[sbuf(phase, f"qT{i}{j}", [P, KD, P], F32R) for j in range(2)] for i in range(2)]
            b.mx = [sbuf(phase, f"mx{i}", [P, HPT]) for i in range(2)]
            b.e = [sbuf(phase, f"e{i}", [P, HPT * P]) for i in range(2)]
            b.et = [sbuf(phase, f"et{i}", [P, 4 * P]) for i in range(2)]
            b.avT = [sbuf(phase, f"avT{i}", [P, 4 * P]) for i in range(2)]
            b.rsum = [sbuf(phase, f"rsum{i}", [P, HEADS // 2]) for i in range(2)]
            b.attn = sbuf(phase, "attn", [P, 2, DIM // 2])
            b.aT = [sbuf(phase, f"aT{i}", [P, KD, P], F32R) for i in range(2)]
            ps = Named()
            ps.scores = [psum(phase, f"scores{i}", 1024) for i in range(2)]
            ps.et = psum(phase, "et_ps", 512)
            ps.av = psum(phase, "av_ps", 512)
            ps.misc_a = psum(phase, "misc_a", 512)
            ps.misc_b = psum(phase, "misc_b", 512)
            attention(nc, sem, c, b, ps, A_x, A_ctx, x1_dram, tiles)

        w = Named()
        w.gu = sbuf(whole, "w_gu", [P, KD, 2 * INTER], F32R)
        w.dn = [sbuf(whole, f"w_dn{i}", [P, KI, DIM], F32R) for i in range(2)]
        b = Named()
        b.x = [sbuf(whole, f"fx{i}", [P, CHUNK, DIM]) for i in range(2)]
        b.z = [sbuf(whole, f"z{i}", [P, DIM]) for i in range(2)]
        b.zT = [[sbuf(whole, f"zT{i}{j}", [P, KD, CHUNK * P], F32R) for j in range(2)] for i in range(2)]
        b.bn = sbuf(whole, "fbn", [P, CHUNK, 6])
        b.mv = sbuf(whole, "fmv", [P, CHUNK, 2])
        b.rstd = sbuf(whole, "frstd", [P, CHUNK])
        b.ssq = sbuf(whole, "ssq", [P, CHUNK])
        b.rrms = sbuf(whole, "rrms", [P, CHUNK])
        z_bank = psum(whole, "z_ps", 512)
        norm = FirstNorm(nc, sem, c, b, z_bank, x1_dram)
        with ExitStack() as scratch:
            tmp = Named()
            tmp.gu_val = sbuf(scratch, "gu_val", [P, 2 * INTER // P, DIM // 8, 4], U32)
            tmp.gu_sgn = sbuf(scratch, "gu_sgn", [P, 2 * INTER // P, DIM // 8], U32)
            tmp.gu_scale = sbuf(scratch, "gu_scale", [KD, 2 * INTER], F16)
            tmp.gu_scale_sorted = sbuf(scratch, "gu_scale_sorted", [KD, 2 * INTER], F16)
            tmp.dn_scale = sbuf(scratch, "dn_scale", [P, KI, DIM], F16)
            tmp.fw = [sbuf(scratch, f"fw{i}", [P, DIM]) for i in range(4)]
            ps = Named()
            ps.fT = [psum(scratch, f"fT{i}", 512) for i in range(4)]
            ps.scales = psum(scratch, "scales_ps", 512)
            ffn_weights(nc, sem, c, w, tmp, ps, norm, A_gus, A_dns)

        b.part = [[[sbuf(whole, f"part{e}{half}{i}", [P, CHUNK * P]) for i in range(3)] for half in range(2)]
                  for e in range(2)]
        b.h = [[sbuf(whole, f"h{a}{i}", [P, CHUNK * P], F32R) for i in range(3)] for a in range(2)]
        b.junk = [sbuf(whole, f"junk{i}", [P, DIM], F16) for i in range(2)]
        ps = Named()
        ps.sums = [psum(whole, f"sums{i}", 512) for i in range(3)]
        ps.z = z_bank
        ps.y = [psum(whole, f"y_ps{i}", 512) for i in range(CHUNK)]
        ffn(nc, sem, c, w, b, ps, norm, out, tiles)


INPUTS = ["x", "ctx_1024", "fside_BxSx2_0", "L0_xattn_Wq", "L0_xattn_Wkv", "L0_xattn_Wout", "L0_xattn_bout",
          "L0_ffn_gate_up_packed", "L0_ffn_gate_up_scales", "L0_ffn_down_packed", "L0_ffn_down_scales"]


def kernel(**inputs):
    import numpy as np
    import concourse.bacc as bacc
    from concourse.bass_utils import run_bass_kernel_spmd

    nc = bacc.Bacc("TRN2", target_bir_lowering=False, num_devices=1, dynamic_dma_scratch_size=1024)
    arrays, args = {}, []
    for name in INPUTS:
        a = np.ascontiguousarray(inputs[name])
        if a.dtype == np.int32:
            a = a.view(np.uint32)
        arrays[f"in_{name}"] = a
        args.append(nc.dram_tensor(f"in_{name}", a.shape, mybir.dt.from_np(a.dtype), kind="ExternalInput").ap())
    out = nc.dram_tensor("out", inputs["x"].shape, F32, kind="ExternalOutput").ap()
    program(nc, *args, out)
    result = run_bass_kernel_spmd(nc, [arrays], core_ids=[0])
    return result.results[0]["out"]
```
